# Optimizing a Trainium2 kernel written in Bass

```python
import numpy as np
import jax
import jax.numpy as jnp

def _softmax(x, axis=-1):
    return jax.nn.softmax(x, axis=axis)

def _gelu(x):
    return jax.nn.gelu(x, approximate=True)

def _silu(x):
    return jax.nn.silu(x)

def _sigmoid(x):
    return jax.nn.sigmoid(x)

def _layernorm(x, axis=-1, eps=1e-05):
    m = jnp.mean(x, axis=axis, keepdims=True)
    v = jnp.var(x, axis=axis, keepdims=True)
    return (x - m) / jnp.sqrt(v + eps)

def _scatter_add(tgt, idx, src, axis=0):
    return tgt.at[idx].add(src)

def _segment_sum(src, seg, n):
    return jax.ops.segment_sum(src, seg, n)
kernel_name = 'mk_adj_resnorm_d4_adj_r2_1453ff'

def setup_inputs(seed: int=0):
    np.random.seed(seed)
    _w = jnp.asarray

    def _rec_inputs():
        import jax
        import jax.numpy as jnp
        _gk = jax.random.key(seed)
        x = -0.0002928 + 1 * jax.random.normal(jax.random.fold_in(_gk, 1), (128, 128, 128), jnp.float32)
        _a = jax.random.bernoulli(jax.random.fold_in(_gk, 2), 0.125, (128, 128))
        _a = jnp.logical_or(_a, jnp.eye(128, dtype=bool))
        _af = _a.astype(jnp.float32)
        _af = _af * jax.random.uniform(jax.random.fold_in(_gk, 3), (128, 128), jnp.float32, 0.05, 1)
        adj = _af
        return (x, adj)
    x, adj = _rec_inputs()

    def _L0_gnn_setup():
        import jax, jax.numpy as jnp
        import numpy as np
        N = 2048
        NFEAT, NHID, NCLASS = (128, 256, 128)
        B = 4

        def _slconv(x, adj, S, W):
            support = jnp.einsum('bnf,fh->bnh', x, W)
            weighting = adj * S
            return jnp.einsum('nm,bmh->bnh', weighting, support)
        key = jax.random.key(seed)
        ks = jax.random.split(key, 6)
        x = jax.random.normal(ks[0], (B, N, NFEAT), dtype=jnp.float32)
        adj = jax.random.uniform(ks[1], (N, N), dtype=jnp.float32)
        S = jnp.ones((N, N), dtype=jnp.float32)
        W1 = jax.random.normal(ks[2], (NFEAT, NHID), dtype=jnp.float32) / np.sqrt(NFEAT)
        W2 = jax.random.normal(ks[3], (NHID, 2 * NHID), dtype=jnp.float32) / np.sqrt(NHID)
        W3 = jax.random.normal(ks[4], (2 * NHID, NCLASS), dtype=jnp.float32) / np.sqrt(2 * NHID)
        return {'x': x, 'adj': adj, 'S': S, 'W1': W1, 'W2': W2, 'W3': W3}
    _L0_gnn_all = _L0_gnn_setup()
    _L0_gnn_in = {k: v for k, v in _L0_gnn_all.items() if k in ('W1', 'W2', 'W3')}
    del _L0_gnn_all

    def _L1_gnn_setup():
        import jax, jax.numpy as jnp
        import numpy as np
        B, T, D, H = (64, 1024, 128, 128)
        MAX_SKIP = 4

        def _lstm_last(Wih, Whh, bih, bhh, xs):
            N, _, Hd = xs.shape
            bias = bih + bhh

            def step(carry, x_t):
                h, c = carry
                g = x_t @ Wih.T + h @ Whh.T + bias
                i, f, gg, o = jnp.split(g, 4, axis=-1)
                c = jax.nn.sigmoid(f) * c + jax.nn.sigmoid(i) * jnp.tanh(gg)
                h = jax.nn.sigmoid(o) * jnp.tanh(c)
                return ((h, c), None)
            init = (jnp.zeros((N, Hd), xs.dtype), jnp.zeros((N, Hd), xs.dtype))
            (h_last, _), _ = jax.lax.scan(step, init, jnp.swapaxes(xs, 0, 1))
            return h_last
        key = jax.random.key(seed)
        ks = jax.random.split(key, 8)
        s = 0.05
        x = jax.random.normal(ks[0], (B, T, D), jnp.float32)
        adj = jax.random.uniform(ks[1], (T, T), jnp.float32) / T
        Wg0 = jax.random.normal(ks[2], (D, H), jnp.float32) * s
        bg0 = jnp.zeros((H,), jnp.float32)
        Wg1 = jax.random.normal(ks[3], (H, H), jnp.float32) * s
        bg1 = jnp.zeros((H,), jnp.float32)
        Wih = jax.random.normal(ks[4], (MAX_SKIP, 4 * H, H), jnp.float32) * s
        Whh = jax.random.normal(ks[5], (MAX_SKIP, 4 * H, H), jnp.float32) * s
        bih = jax.random.normal(ks[6], (MAX_SKIP, 4 * H), jnp.float32) * s
        bhh = jax.random.normal(ks[7], (MAX_SKIP, 4 * H), jnp.float32) * s
        return dict(x=x, adj=adj, Wg0=Wg0, bg0=bg0, Wg1=Wg1, bg1=bg1, Wih=Wih, Whh=Whh, bih=bih, bhh=bhh)
    _L1_gnn_all = _L1_gnn_setup()
    _L1_gnn_in = {k: v for k, v in _L1_gnn_all.items() if k in ('Wg0', 'bg0', 'Wg1', 'bg1', 'Wih', 'Whh', 'bih', 'bhh')}
    del _L1_gnn_all

    def _L2_gnn_setup():
        import jax, jax.numpy as jnp
        import numpy as np
        ALPHA = 0.2
        key = jax.random.key(seed)
        k1, k2, k3, k4 = jax.random.split(key, 4)
        B, N, Fin, Fout = (8, 1024, 128, 128)
        h = jax.random.normal(k1, (B, N, Fin), dtype=jnp.float32)
        adj = jax.random.randint(k2, (N, N), 0, 2).astype(jnp.float32)
        adj = jnp.maximum(adj, jnp.eye(N, dtype=jnp.float32))

        def xavier(k, shape, gain=1.414):
            fan_in, fan_out = (shape[0], shape[1])
            a = gain * np.sqrt(6.0 / (fan_in + fan_out))
            return jax.random.uniform(k, shape, dtype=jnp.float32, minval=-a, maxval=a)
        W = xavier(k3, (Fin, Fout))
        a = xavier(k4, (2 * Fout, 1))
        return {'h': h, 'adj_matrix': adj, 'W': W, 'a': a}
    _L2_gnn_all = _L2_gnn_setup()
    _L2_gnn_in = {k: v for k, v in _L2_gnn_all.items() if k in ('W', 'a')}
    del _L2_gnn_all

    def _L3_gnn_setup():
        import jax, jax.numpy as jnp
        import numpy as np
        EPS = 1e-05

        def _batchnorm(x, gamma, beta):
            mu = jnp.mean(x, axis=0)
            var = jnp.var(x, axis=0)
            return (x - mu) * jax.lax.rsqrt(var + EPS) * gamma + beta
        key = jax.random.key(seed)
        ks = jax.random.split(key, 4)
        b, n, d, h, o = (32, 1024, 128, 256, 128)
        features = jax.random.normal(ks[0], (b, n, d), dtype=jnp.float32)
        A = jax.random.uniform(ks[1], (n, n), dtype=jnp.float32)
        lim1 = float(np.sqrt(6.0 / (d + h)))
        W1 = jax.random.uniform(ks[2], (h, d), minval=-lim1, maxval=lim1, dtype=jnp.float32)
        b1 = jnp.zeros((h,), jnp.float32)
        lim2 = float(np.sqrt(6.0 / (h + o)))
        W2 = jax.random.uniform(ks[3], (o, h), minval=-lim2, maxval=lim2, dtype=jnp.float32)
        b2 = jnp.zeros((o,), jnp.float32)
        g1 = jnp.ones((h,), jnp.float32)
        be1 = jnp.zeros((h,), jnp.float32)
        g2 = jnp.ones((o,), jnp.float32)
        be2 = jnp.zeros((o,), jnp.float32)
        return {'features': features, 'A': A, 'W1': W1, 'b1': b1, 'g1': g1, 'be1': be1, 'W2': W2, 'b2': b2, 'g2': g2, 'be2': be2}
    _L3_gnn_all = _L3_gnn_setup()
    _L3_gnn_in = {k: v for k, v in _L3_gnn_all.items() if k in ('W1', 'b1', 'g1', 'be1', 'W2', 'b2', 'g2', 'be2')}
    del _L3_gnn_all
    return {'x': x, 'adj': adj, 'L0_gnn_W1': _L0_gnn_in['W1'], 'L0_gnn_W2': _L0_gnn_in['W2'], 'L0_gnn_W3': _L0_gnn_in['W3'], 'L1_gnn_Wg0': _L1_gnn_in['Wg0'], 'L1_gnn_bg0': _L1_gnn_in['bg0'], 'L1_gnn_Wg1': _L1_gnn_in['Wg1'], 'L1_gnn_bg1': _L1_gnn_in['bg1'], 'L1_gnn_Wih': _L1_gnn_in['Wih'], 'L1_gnn_Whh': _L1_gnn_in['Whh'], 'L1_gnn_bih': _L1_gnn_in['bih'], 'L1_gnn_bhh': _L1_gnn_in['bhh'], 'L2_gnn_W': _L2_gnn_in['W'], 'L2_gnn_a': _L2_gnn_in['a'], 'L3_gnn_W1': _L3_gnn_in['W1'], 'L3_gnn_b1': _L3_gnn_in['b1'], 'L3_gnn_g1': _L3_gnn_in['g1'], 'L3_gnn_be1': _L3_gnn_in['be1'], 'L3_gnn_W2': _L3_gnn_in['W2'], 'L3_gnn_b2': _L3_gnn_in['b2'], 'L3_gnn_g2': _L3_gnn_in['g2'], 'L3_gnn_be2': _L3_gnn_in['be2']}

def reference(x, adj, L0_gnn_W1, L0_gnn_W2, L0_gnn_W3, L1_gnn_Wg0, L1_gnn_bg0, L1_gnn_Wg1, L1_gnn_bg1, L1_gnn_Wih, L1_gnn_Whh, L1_gnn_bih, L1_gnn_bhh, L2_gnn_W, L2_gnn_a, L3_gnn_W1, L3_gnn_b1, L3_gnn_g1, L3_gnn_be1, L3_gnn_W2, L3_gnn_b2, L3_gnn_g2, L3_gnn_be2):
    import jax
    import jax.numpy as jnp

    def _L0_gnn_ref(x, adj, S, W1, W2, W3):
        import jax, jax.numpy as jnp
        import numpy as np
        N = 2048
        NFEAT, NHID, NCLASS = (128, 256, 128)
        B = 4

        def _slconv(x, adj, S, W):
            support = jnp.einsum('bnf,fh->bnh', x, W)
            weighting = adj * S
            return jnp.einsum('nm,bmh->bnh', weighting, support)
        h = jax.nn.relu(_slconv(x, adj, S, W1))
        h = jax.nn.relu(_slconv(h, adj, S, W2))
        return _slconv(h, adj, S, W3)

    def _L1_gnn_ref(x, adj, Wg0, bg0, Wg1, bg1, Wih, Whh, bih, bhh):
        import jax, jax.numpy as jnp
        import numpy as np
        B, T, D, H = (64, 1024, 128, 128)
        MAX_SKIP = 4

        def _lstm_last(Wih, Whh, bih, bhh, xs):
            N, _, Hd = xs.shape
            bias = bih + bhh

            def step(carry, x_t):
                h, c = carry
                g = x_t @ Wih.T + h @ Whh.T + bias
                i, f, gg, o = jnp.split(g, 4, axis=-1)
                c = jax.nn.sigmoid(f) * c + jax.nn.sigmoid(i) * jnp.tanh(gg)
                h = jax.nn.sigmoid(o) * jnp.tanh(c)
                return ((h, c), None)
            init = (jnp.zeros((N, Hd), xs.dtype), jnp.zeros((N, Hd), xs.dtype))
            (h_last, _), _ = jax.lax.scan(step, init, jnp.swapaxes(xs, 0, 1))
            return h_last
        h = jax.nn.relu(jnp.einsum('ts,bsh->bth', adj, x @ Wg0 + bg0))
        h = jax.nn.relu(jnp.einsum('ts,bsh->bth', adj, h @ Wg1 + bg1))
        Bv, Tv, Hd = h.shape
        for p in range(1, MAX_SKIP + 1):
            nw = Tv // p
            wins = h[:, :nw * p, :].reshape(Bv * nw, p, Hd)
            last = _lstm_last(Wih[p - 1], Whh[p - 1], bih[p - 1], bhh[p - 1], wins)
            idx = jnp.arange(nw) * p + (p - 1)
            h = h.at[:, idx, :].set(last.reshape(Bv, nw, Hd))
        return h

    def _L2_gnn_ref(h, adj_matrix, W, a):
        import jax, jax.numpy as jnp
        import numpy as np
        ALPHA = 0.2
        Fout = W.shape[1]
        Wh = jnp.einsum('bnf,fo->bno', h, W)
        a1, a2 = (a[:Fout, 0], a[Fout:, 0])
        s1 = Wh @ a1
        s2 = Wh @ a2
        e = s1[:, :, None] + s2[:, None, :]
        e = jnp.where(e >= 0, e, ALPHA * e)
        e = jnp.where(adj_matrix[None] == 0, -jnp.inf, e)
        attention = jax.nn.softmax(e, axis=-1)
        h_prime = jnp.einsum('bij,bjo->bio', attention, Wh)
        return h_prime

    def _L3_gnn_ref(features, A, W1, b1, g1, be1, W2, b2, g2, be2):
        import jax, jax.numpy as jnp
        import numpy as np
        EPS = 1e-05

        def _batchnorm(x, gamma, beta):
            mu = jnp.mean(x, axis=0)
            var = jnp.var(x, axis=0)
            return (x - mu) * jax.lax.rsqrt(var + EPS) * gamma + beta
        b, n, d = features.shape
        A_norm = A + jnp.eye(n, dtype=A.dtype)
        deg = jnp.sum(A_norm, axis=0) + jnp.sum(A_norm, axis=1) - jnp.diagonal(A_norm)
        dinv = jax.lax.rsqrt(deg)
        A_hat = A_norm * dinv[:, None] * dinv[None, :]
        agg = jnp.einsum('nm,bmd->bnd', A_hat, features)
        x = agg.reshape(-1, d)
        h = jax.nn.relu(_batchnorm(x @ W1.T + b1, g1, be1))
        out = h @ W2.T + b2
        out = _batchnorm(out, g2, be2)
        return out.reshape(b, n, -1)
    x = _layernorm(x + _L0_gnn_ref(x, adj, adj, L0_gnn_W1, L0_gnn_W2, L0_gnn_W3), axis=-1)
    x = _layernorm(x + _L1_gnn_ref(x, adj, L1_gnn_Wg0, L1_gnn_bg0, L1_gnn_Wg1, L1_gnn_bg1, L1_gnn_Wih, L1_gnn_Whh, L1_gnn_bih, L1_gnn_bhh), axis=-1)
    x = _layernorm(x + _L2_gnn_ref(x, adj, L2_gnn_W, L2_gnn_a), axis=-1)
    x = _layernorm(x + _L3_gnn_ref(x, adj, L3_gnn_W1, L3_gnn_b1, L3_gnn_g1, L3_gnn_be1, L3_gnn_W2, L3_gnn_b2, L3_gnn_g2, L3_gnn_be2), axis=-1)
    return x

_drawn_inputs = setup_inputs


def setup_inputs(seed=0):
    import zlib

    import numpy as np

    out = dict(_drawn_inputs(seed))
    spreads = {'L1_gnn_bg0': (0.0, 0.1),
     'L1_gnn_bg1': (0.0, 0.1),
     'L3_gnn_b1': (0.0, 0.8),
     'L3_gnn_g1': (1.0, 0.2),
     'L3_gnn_be1': (0.0, 0.1),
     'L3_gnn_b2': (0.0, 0.8),
     'L3_gnn_g2': (1.0, 0.2),
     'L3_gnn_be2': (0.0, 0.1)}
    factors = {'L1_gnn_Whh': 8.0, 'L1_gnn_bih': 4.474, 'L1_gnn_bhh': 4.098}
    for name, (base, spread) in spreads.items():
        noise = np.random.default_rng([zlib.crc32(name.encode()), seed]).standard_normal(out[name].shape)
        drawn = base * np.exp(spread * noise) if base else spread * noise
        out[name] = jnp.asarray(drawn.astype(out[name].dtype))
    for name, factor in factors.items():
        out[name] = (out[name] * factor).astype(out[name].dtype)
    return out
```

```python
import concourse.bass as bass
from concourse import mybir
from contextlib import ExitStack

B, N, D = 128, 128, 128
BH = 4
COLS = BH * N
UB = 2 * BH
UNITS = B // UB
GROUPS = B // BH
HID1, HID2 = 256, 512
SKIPS = 4
EPS = 1e-5
ALPHA = 0.2
MASKED = -1.0e30
GATE_I, GATE_F, GATE_G, GATE_O = range(4)

SLOTS = [(1, 0, 0, BH), (1, 0, BH, BH)] + [(p, s, 0, UB) for p in range(2, SKIPS + 1) for s in range(p)]
NSLOT = len(SLOTS)


def slot_gates(s):
    return [GATE_I, GATE_G, GATE_O] if SLOTS[s][1] == 0 else [GATE_I, GATE_G, GATE_F, GATE_O]


GATES_BEFORE = [sum(len(slot_gates(k)) for k in range(s)) for s in range(NSLOT + 1)]
LATER_BEFORE = [sum(SLOTS[k][1] > 0 for k in range(s)) for s in range(NSLOT + 1)]

ORDER = [
    ("backT", 0), ("backT", 1),
    ("gates", 0), ("ax", 0), ("tanhc", 0), ("ax", 1), ("hout", 0), ("norm2", 0), ("h1", 0), ("norm2", 1),
    ("gates", 1), ("x2T", 0), ("tanhc", 1), ("x2T", 1), ("hout", 1), ("h1", 1), ("ah1", 0),
    ("gates", 2), ("wh", 0), ("tanhc", 2), ("s2", 0), ("hout", 2), ("wh", 1), ("s2", 1), ("lrelu", 0), ("ah1", 1),
    ("rowmax", 0), ("lrelu", 1), ("rowmax", 1),
    ("gates", 3), ("h2a", 0), ("tanhc", 3), ("expo", 0), ("hout", 3), ("h2b", 0), ("expo", 1),
    ("gates", 4), ("pT", 0), ("tanhc", 4), ("pT", 1), ("hout", 4), ("z", 0),
    ("gates", 5), ("h2a", 1), ("tanhc", 5), ("hout", 5),
    ("gates", 6), ("att", 0), ("tanhc", 6), ("hout", 6), ("att", 1), ("h2b", 1),
    ("gates", 7), ("oz", 0), ("tanhc", 7), ("hout", 7), ("norm3", 0), ("z", 1), ("norm3", 1),
    ("gates", 8), ("agg", 0), ("tanhc", 8), ("agg", 1), ("hout", 8), ("oz", 1), ("norm1", 0),
    ("gates", 9), ("stat", 0), ("tanhc", 9), ("gax", 0), ("hout", 9), ("norm1", 1), ("stat", 1),
    ("gates", 10), ("gax", 1), ("tanhc", 10), ("gh", 0), ("hout", 10), ("gh", 1), ("gah", 0), ("gah", 1),
    ("gx", 0), ("gx", 1),
]
FILLS = {"ax": 1, "h1": 2, "ah1": 2, "h2a": 2, "h2b": 2, "z": 1, "oz": 1, "gax": 1, "gh": 1, "gah": 1, "gx": 1,
         "backT": 1, "x2T": 1, "wh": 2, "s2": 1, "pT": 1, "att": 1, "agg": 1, "stat": 2}
LAG = {s: 0 for s in ("ax", "h1", "ah1", "h2a", "h2b", "z", "oz", "norm1", "gax", "gh", "gah", "gx")}
LAG |= {s: 1 for s in ("gates", "tanhc", "hout")}
LAG |= {s: 2 for s in ("backT", "norm2", "x2T", "wh", "s2", "lrelu", "rowmax", "expo", "pT", "att", "norm3",
                       "agg", "stat")}
NBANK = 4
SETUP_STEPS = 19
BODIES = UNITS + 2
LOOP0, LOOP1 = 3, UNITS


def active(step, t):
    return 0 <= t - LAG[step] < UNITS


FILL_LIST = [(s, h, j) for s, h in ORDER if s in FILLS for j in range(FILLS[s])]
BANK = {f: i % NBANK for i, f in enumerate(FILL_LIST)}
PER_BODY = [sum(BANK[f] == k for f in FILL_LIST) for k in range(NBANK)]


def fills_in(t, bank, upto=None):
    n = 0
    for f in FILL_LIST:
        if f == upto:
            break
        n += BANK[f] == bank and active(f[0], t)
    return n


def fill_number(f, t):
    bank = BANK[f]
    if isinstance(t, int):
        return sum(fills_in(q, bank) for q in range(t)) + fills_in(t, bank, f) + 1
    base = sum(fills_in(q, bank) for q in range(LOOP0)) + fills_in(LOOP0, bank, f) + 1
    return (t - LOOP0) * PER_BODY[bank] + base


def fill_before(f, t):
    q, at = (t, t) if isinstance(t, int) else (LOOP0, t)
    while q >= 0:
        here = [e for e in FILL_LIST if BANK[e] == BANK[f] and active(e[0], q)]
        if f in here and at is t:
            here = here[:here.index(f)]
        if here:
            return here[-1], at
        q, at = q - 1, at - 1
    return None


def build_adj_resnorm_d4(nc, x, adj, adjT, l0_w1, l0_w2, l0_w3, l1_wg0, l1_bg0, l1_wg1, l1_bg1, l1_wihT, l1_whhT,
                         l1_bih, l1_bhh, l2_w, l2_wT, l2_a, l3_w1T, l3_vec1, l3_w2T, l3_vec2, eye, out):
    fp32 = mybir.dt.float32
    ALU = mybir.AluOpType
    ACT = mybir.ActivationFunctionType
    AX = mybir.AxisListType
    V = nc.vector

    ctx = ExitStack()
    with ctx:
        def sb(name, shape, dt=fp32, where=ctx):
            return where.enter_context(nc.sbuf_tensor(name, shape, dt))

        def sem(name):
            return ctx.enter_context(nc.semaphore(name))

        A_ = sb("A_", [128, N])
        AT = sb("AT", [128, N])
        ANT = sb("ANT", [128, N])
        A2T = sb("A2T", [128, N])
        AHT = sb("AHT", [128, N])
        I_ = sb("I_", [128, 128])
        maskadd = sb("maskadd", [128, N])
        w1 = sb("w1", [128, HID1])
        w2 = sb("w2", [128, 2, HID2])
        w3 = sb("w3", [128, 4, D])
        wg0 = sb("wg0", [128, D])
        wg1 = sb("wg1", [128, D])
        bg = sb("bg", [1, 2, D])
        rs = sb("rs", [1, BH, N])
        wih = sb("wih", [128, SKIPS, 4 * D])
        whh = sb("whh", [128, SKIPS, 4 * D])
        gbias = sb("gbias", [128, SKIPS, 4])
        bhh = sb("bhh", [128, SKIPS, 4])
        w_l2 = sb("w_l2", [128, D])
        w_l2T = sb("w_l2T", [128, D])
        a12 = sb("a12", [128, 2])
        wa1 = sb("wa1", [128, 1])
        wa2 = sb("wa2", [128, 128])
        w1T_l3 = sb("w1T_l3", [128, HID1])
        w2T_l3 = sb("w2T_l3", [128, 2, D])
        vec1 = sb("vec1", [128, 3, 2])
        vec2 = sb("vec2", [128, 3, 1])
        ones = sb("ones", [128, 128])
        scratch = sb("scratch", [128, 128])
        deg = sb("deg", [128, 4])
        dinv = sb("dinv", [128, 1])
        eps4 = sb("eps4", [128, BH])
        mhalf = sb("mhalf", [128, BH])
        AGG = sb("AGG", [128, GROUPS, COLS])
        stats1 = sb("stats1", [128, 2, GROUPS, 6])
        stats2 = sb("stats2", [128, GROUPS, 6])
        bn = sb("bn", [128, 16])
        lnst = sb("lnst", [128, 3, 2, BH, 6])
        lnmv = sb("lnmv", [128, 3, 2, BH, 2])
        lnve = sb("lnve", [128, 3, 2, BH])
        lnr = sb("lnr", [128, 3, 2, BH])
        carry = sb("carry", [128, 1])
        s1 = sb("s1", [128, 2, BH])
        nmax = sb("nmax", [128, 2, BH])
        psum_ = sb("psum_", [128, 2, BH])
        rsum = sb("rsum", [128, 2, BH])

        fused = ExitStack()
        with fused:
            def fb(name, shape):
                return sb(name, shape, fp32, fused)

            xin = fb("xin", [128, 2, BH, D])
            yT = fb("yT", [128, 2, BH, N])
            h1 = fb("h1", [128, 2, BH, HID1])
            y2T = fb("y2T", [128, 2, 2, BH, N])
            h2T = fb("h2T", [128, 4, BH, N])
            z = fb("z", [128, 2, BH, D])
            x1 = fb("x1", [128, 2, BH, D])
            xl = fb("xl", [128, UB, N])
            x2 = fb("x2", [128, 2, BH, D])
            x2T = fb("x2T", [128, 2, BH, N])
            wh = fb("wh", [128, 2, BH, D])
            E = fb("E", [128, 2, BH, N])
            P = fb("P", [128, 2, BH, N])
            PT = fb("PT", [128, 2, BH, N])
            x3 = fb("x3", [128, 2, BH, D])
            gact = fb("gact", [128, 4, COLS])
            cell = fb("cell", [128, COLS])
            fterm = fb("fterm", [128, COLS])
            iterm = fb("iterm", [128, COLS])
            tanhc = fb("tanhc", [128, COLS])
            hs = fb("hs", [128, COLS])
            HT = fb("HT", [128, UB, N])
        X3 = sb("X3", [128, GROUPS, COLS])
        relu = sb("relu", [128, 2, 2, COLS])
        oaff = sb("oaff", [128, 2, COLS])
        res = sb("res", [128, 2, BH, D])
        fin = sb("fin", [128, 2, BH, D])

        G = ctx.enter_context(nc.psum_tensor("G", [128, 4, COLS], fp32))
        F = ctx.enter_context(nc.psum_tensor("F", [128, NBANK, COLS], fp32))
        x3_dram = nc.dram_tensor("x3_dram", (GROUPS, 128, COLS), fp32, kind="Internal").ap()

        loaded = sem("weights_loaded")
        eye_loaded = sem("eye_loaded")
        filled = [sem(f"bank{k}_filled") for k in range(NBANK)]
        x_loaded = [sem(f"x_half{h}_loaded") for h in range(2)]
        names = ["yT", "h1_0", "h1_1", "y2T_0", "y2T_1", "h2T_0", "h2T_1", "h2T_2", "h2T_3", "z", "r1", "x1",
                 "x1_kept", "gyT", "gh1", "gy2T", "xl", "r2", "x2", "x2T", "wh", "s1", "E", "L", "nmax", "P",
                 "rsum", "PT", "r3", "x3", "agg", "stat"]
        ready = {n: sem(f"{n}_ready") for n in names}
        h2T_read = sem("h2T_read")
        added = [sem(f"ln{n}_added") for n in range(3)]
        stated = [sem(f"ln{n}_stats") for n in range(3)]
        aggregated = [sem(f"ln{n}_mean_var") for n in range(3)]
        eps_added = [sem(f"ln{n}_eps_added") for n in range(3)]
        rstd = [sem(f"ln{n}_rstd") for n in range(3)]
        gates_filled = sem("gates_filled")
        gates_done = sem("gates_done")
        terms_done = sem("cell_terms_done")
        cell_ready = sem("cell_ready")
        tanhc_ready = sem("tanhc_ready")
        h_ready = sem("lstm_h_ready")
        x3_stored = [sem(f"x3_half{h}_stored") for h in range(2)]
        setup_dve = sem("setup_dve")
        setup_pe = sem("setup_pe")
        setup_pool = sem("setup_pool")
        setup_act = sem("setup_act")
        bn_dve = sem("bn_dve")
        deg_sum, shift_term = sem("deg_sum"), sem("shift_term")
        bn_pool = sem("bn_pool")
        hpre_filled = sem("hpre_filled")
        relu_ready = sem("relu_ready")
        out_filled = sem("out_filled")
        out_kept = sem("out_kept")
        x3_back = sem("x3_back")
        affine_ready = sem("affine_ready")
        rows_filled = sem("rows_filled")
        res_ready = sem("residual_ready")
        f_stats, f_mv, f_eps, f_rstd = sem("fin_stats"), sem("fin_mean_var"), sem("fin_eps_added"), sem("fin_rstd")
        fin_ready = sem("fin_ready")
        stored = [sem(f"out_par{h}_stored") for h in range(2)]

        LOADS = [(A_, adj), (AT, adjT), (I_, eye), (w1, l0_w1), (w2, l0_w2), (w3, l0_w3), (wg0, l1_wg0),
                 (wg1, l1_wg1), (bg[:, 0, :], l1_bg0), (bg[:, 1, :], l1_bg1), (wih, l1_wihT), (whh, l1_whhT),
                 (gbias, l1_bih), (bhh, l1_bhh), (w_l2, l2_w), (w_l2T, l2_wT), (a12, l2_a),
                 (w1T_l3, l3_w1T), (w2T_l3, l3_w2T), (vec1, l3_vec1), (vec2, l3_vec2)]
        NLOAD = 16 * len(LOADS)

        def wait(eng, s, n):
            if not isinstance(n, int) or n > 0:
                eng.wait_ge(s, n)

        def bodies(eng, body):
            for t in range(LOOP0):
                body(t)
            with eng.Fori(LOOP0, LOOP1) as t:
                body(t)
            for t in range(LOOP1, BODIES):
                body(t)

        def present(step, t):
            return not isinstance(t, int) or active(step, t)

        def half_number(step, t, h):
            return (t - LAG[step]) * 2 + h

        def bank_of(step, h, j=0):
            return F[:, BANK[(step, h, j)], :]

        def wait_filled(eng, step, h, t, j=0):
            f = (step, h, j)
            eng.wait_ge(filled[BANK[f]], fill_number(f, t))

        PRODUCT = {"ax": "yT", "z": "z", "gax": "gyT", "gh": "gh1", "gah": "gy2T", "gx": "xl", "x2T": "x2T",
                   "s2": "E", "pT": "PT", "agg": "agg"}
        PRODUCTS = {"h1": ("h1_0", "h1_1"), "ah1": ("y2T_0", "y2T_1"), "h2a": ("h2T_0", "h2T_1"),
                    "h2b": ("h2T_2", "h2T_3"), "wh": ("wh", "s1")}
        SUMS = {"oz": 0, "backT": 1, "att": 2}

        def read_signal(f, t):
            step, h, j = f
            n = half_number(step, t, h)
            if step == "stat":
                return ready["stat"], 2 * n + j + 1
            if step in SUMS:
                return added[SUMS[step]], n + 1
            return ready[PRODUCT[step] if step in PRODUCT else PRODUCTS[step][j]], n + 1

        def per_batch(ap):
            return ap.rearrange("p (b n) -> p b n", b=BH)

        block = ctx.enter_context(nc.Block())

        @block.sync
        def _(sp):
            for h in range(2):
                sp.dma_start(xin[:, h], x[h]).then_inc(x_loaded[h], 16)
            for dst, src in LOADS:
                sp.dma_start(dst[:] if dst.__class__ is not bass.AP else dst, src).then_inc(loaded, 16)

            def body(t):
                for step, h in ORDER:
                    if not present(step, t):
                        continue
                    if step == "oz" and (not isinstance(t, int) or t + 1 < UNITS):
                        sp.wait_ge(added[0], half_number(step, t, h) + 1)
                        sp.dma_start(xin[:, h], x[(t + 1) * 2 + h]).then_inc(x_loaded[h], 16)
                    if step == "norm3":
                        sp.wait_ge(ready["x3"], half_number(step, t, h) + 1)
                        sp.dma_start(x3_dram[half_number(step, t, h)],
                                     x3[:, h]).then_inc(x3_stored[h], 16)

            for t in range(LOOP0):
                body(t)
            with sp.Fori(LOOP0, LOOP1 - 1) as t:
                body(t)
            for t in range(LOOP1 - 1, BODIES):
                body(t)

            sp.wait_ge(ready["stat"], 4 * UNITS)
            for h in range(2):
                sp.wait_ge(x3_stored[h], 16 * UNITS)
            parts = 8
            q = GROUPS // parts
            for i in range(parts):
                sp.dma_start(X3[:, i * q:(i + 1) * q, :],
                             x3_dram[i * q:(i + 1) * q].rearrange("g p c -> p g c")).then_inc(x3_back, 16)

            def store(g, par):
                sp.wait_ge(fin_ready, g + 1)
                sp.dma_start(out[g], fin[:, par]).then_inc(stored[par], 16)

            with sp.Fori(0, GROUPS - 1, 2) as g:
                store(g, 0)
                store(g + 1, 1)
            for par in range(2):
                sp.wait_ge(stored[par], 16 * (GROUPS // 2))

        @block.gpsimd
        def _(pool):
            pool.memset(eps4[:], EPS).then_inc(setup_pool, 1)
            pool.memset(mhalf[:], -0.5).then_inc(setup_pool, 1)
            pool.memset(ones[:], 1.0).then_inc(setup_pool, 1)
            pool.wait_ge(setup_pool, 3)
            pool.wait_ge(setup_dve, 7)
            pool.tensor_tensor(dinv[:], deg[:, 3:4], mhalf[:, 0:1], ALU.pow).then_inc(setup_pool, 1)

            def make_rstd(n, h, count):
                pool.wait_ge(aggregated[n], count)
                pool.tensor_tensor(lnve[:, n, h, :], lnmv[:, n, h, :, 1], eps4[:], ALU.add).then_inc(eps_added[n], 1)
                pool.wait_ge(eps_added[n], count)
                pool.tensor_tensor(lnr[:, n, h, :], lnve[:, n, h, :], mhalf[:], ALU.pow).then_inc(rstd[n], 1)

            def body(t):
                for step, h in ORDER:
                    if not present(step, t):
                        continue
                    if step == "oz":
                        make_rstd(0, h, half_number(step, t, h) + 1)
                    if step == "backT":
                        make_rstd(1, h, half_number(step, t, h) + 1)
                    if step == "att":
                        make_rstd(2, h, half_number(step, t, h) + 1)
                    if step == "norm1":
                        n = half_number(step, t, h)
                        pool.wait_ge(setup_pool, 4)
                        pool.wait_ge(ready["x1"], n + 1)
                        pool.tensor_copy(AGG[:, n, :],
                                         x1[:, h].rearrange("p b d -> p (b d)")).then_inc(ready["x1_kept"], 1)

            bodies(pool, body)

            pool.wait_ge(bn_dve, 3)
            pool.tensor_tensor(bn[:, 4:6], bn[:, 2:4], mhalf[:, 0:2], ALU.pow).then_inc(bn_pool, 1)
            pool.wait_ge(bn_dve, 10)
            pool.tensor_tensor(bn[:, 12:13], bn[:, 11:12], mhalf[:, 0:1], ALU.pow).then_inc(bn_pool, 1)

            def fin_rstd(g, par):
                pool.wait_ge(f_mv, g + 1)
                pool.tensor_tensor(lnve[:, 0, par, :], lnmv[:, 0, par, :, 1], eps4[:], ALU.add).then_inc(f_eps, 1)
                pool.wait_ge(f_eps, g + 1)
                pool.tensor_tensor(lnr[:, 0, par, :], lnve[:, 0, par, :], mhalf[:], ALU.pow).then_inc(f_rstd, 1)

            with pool.Fori(0, GROUPS - 1, 2) as g:
                fin_rstd(g, 0)
                fin_rstd(g + 1, 1)

        @block.tensor
        def _(pe):
            mm = pe.matmul
            pe.wait_ge(loaded, NLOAD)
            pe.wait_ge(setup_pool, 3)
            mm(F[0:1, 0, 0:N], ones[:, 0:1], AT[:], start=True, stop=True).then_inc(setup_pe, 1)
            mm(F[:, 1, 0:1], w_l2T[:], a12[:, 0:1], start=True, stop=True).then_inc(setup_pe, 1)
            mm(F[:, 2, 0:128], w_l2T[:], a12[:, 1:2].to_broadcast([128, 128]),
               start=True, stop=True).then_inc(setup_pe, 1)
            pe.wait_ge(setup_dve, 8)
            mm(F[:, 3, 0:N], ones[:], scratch[:], start=True, stop=True).then_inc(setup_pe, 1)
            pe.wait_ge(setup_dve, SETUP_STEPS)

            def fill(step, h, t, j=0):
                f = (step, h, j)
                before = fill_before(f, t)
                if before:
                    pe.wait_ge(*read_signal(*before))
                return F[:, BANK[f], :]

            def full(step, h, j=0):
                return filled[BANK[(step, h, j)]]

            def fused_step(step, h, t):
                n = half_number(step, t, h) if step != "gates" else None
                if step == "ax":
                    pe.wait_ge(x_loaded[h], (t - LAG[step]) * 16 + 16)
                    o = per_batch(fill(step, h, t))
                    for b in range(BH):
                        i = mm(o[:, b, :], xin[:, h, b, :], A2T[:], start=True, stop=True)
                    i.then_inc(full(step, h), 1)
                if step == "h1":
                    pe.wait_ge(ready["yT"], n + 1)
                    for j in range(2):
                        o = fill(step, h, t, j).rearrange("p (b f) -> p b f", b=2)
                        for b in range(2):
                            i = mm(o[:, b, :], yT[:, h, 2 * j + b, :], w1[:], start=True, stop=True)
                        i.then_inc(full(step, h, j), 1)
                if step == "ah1":
                    pe.wait_ge(ready["h1_0"], n + 1)
                    pe.wait_ge(ready["h1_1"], n + 1)
                    for k in range(2):
                        o = per_batch(fill(step, h, t, k))
                        for b in range(BH):
                            i = mm(o[:, b, :], h1[:, h, b, k * 128:(k + 1) * 128], A2T[:], start=True, stop=True)
                        i.then_inc(full(step, h, k), 1)
                if step in ("h2a", "h2b"):
                    for j in range(2):
                        c = j + 2 * (step == "h2b")
                        o = per_batch(fill(step, h, t, j))
                        for k in range(2):
                            if c == 0:
                                pe.wait_ge(ready[f"y2T_{k}"], n + 1)
                            i = mm(o, w2[:, k, c * 128:(c + 1) * 128], y2T[:, h, k], start=(k == 0), stop=(k == 1))
                        i.then_inc(full(step, h, j), 1)
                if step == "z":
                    o = per_batch(fill(step, h, t))
                    for c in range(4):
                        pe.wait_ge(ready[f"h2T_{c}"], n + 1)
                    for b in range(BH):
                        for c in range(4):
                            i = mm(o[:, b, :], h2T[:, c, b, :], w3[:, c, :], start=(c == 0), stop=(c == 3))
                    i.then_inc(full(step, h), 1)
                if step == "oz":
                    pe.wait_ge(ready["z"], n + 1)
                    mm(per_batch(fill(step, h, t)), A2T[:], z[:, h], start=True, stop=True)\
                        .then_inc(full(step, h), 1)
                if step == "gax":
                    pe.wait_ge(ready["x1"], n + 1)
                    o = per_batch(fill(step, h, t))
                    for b in range(BH):
                        i = mm(o[:, b, :], x1[:, h, b, :], AT[:], start=True, stop=True)
                    i.then_inc(full(step, h), 1)
                if step == "gh":
                    pe.wait_ge(ready["gyT"], n + 1)
                    o = per_batch(fill(step, h, t))
                    mm(o, rs[0:1, 0, :], bg[0:1, 0:1, :].to_broadcast([1, BH, D]), start=True, stop=False,
                       skip_group_check=True)
                    for b in range(BH):
                        i = mm(o[:, b, :], yT[:, h, b, :], wg0[:], start=False, stop=(b == BH - 1),
                               skip_group_check=True)
                    i.then_inc(full(step, h), 1)
                if step == "gah":
                    pe.wait_ge(ready["gh1"], n + 1)
                    o = per_batch(fill(step, h, t))
                    for b in range(BH):
                        i = mm(o[:, b, :], h1[:, h, b, 0:D], AT[:], start=True, stop=True)
                    i.then_inc(full(step, h), 1)
                if step == "gx":
                    pe.wait_ge(ready["gy2T"], n + 1)
                    o = per_batch(fill(step, h, t))
                    mm(o, bg[0:1, 1, :], rs[:], start=True, stop=False)
                    mm(o, wg1[:], y2T[:, h, 0], start=False, stop=True).then_inc(full(step, h), 1)
                if step == "gates":
                    lstm_gates(h, t)
                if step == "backT":
                    pe.wait_ge(h_ready, (t - LAG[step]) * NSLOT + NSLOT)
                    o = per_batch(fill(step, h, t))
                    for b in range(BH):
                        i = pe.transpose(o[:, b, :], HT[:, BH * h + b, :], I_[:])
                    i.then_inc(full(step, h), 1)
                if step == "x2T":
                    pe.wait_ge(ready["x2"], n + 1)
                    o = per_batch(fill(step, h, t))
                    for b in range(BH):
                        i = pe.transpose(o[:, b, :], x2[:, h, b, :], I_[:])
                    i.then_inc(full(step, h), 1)
                if step == "wh":
                    pe.wait_ge(ready["x2T"], n + 1)
                    o = per_batch(fill(step, h, t))
                    for b in range(BH):
                        i = mm(o[:, b, :], x2T[:, h, b, :], w_l2[:], start=True, stop=True)
                    i.then_inc(full(step, h), 1)
                    o = fill(step, h, t, 1)
                    for b in range(BH):
                        i = mm(o[:, b:b + 1], x2T[:, h, b, :], wa1[:], start=True, stop=True)
                    i.then_inc(full(step, h, 1), 1)
                if step == "s2":
                    mm(per_batch(fill(step, h, t)), wa2[:], x2T[:, h], start=True, stop=True)\
                        .then_inc(full(step, h), 1)
                if step == "pT":
                    pe.wait_ge(ready["P"], n + 1)
                    o = per_batch(fill(step, h, t))
                    for b in range(BH):
                        i = pe.transpose(o[:, b, :], P[:, h, b, :], I_[:])
                    i.then_inc(full(step, h), 1)
                if step == "att":
                    pe.wait_ge(ready["PT"], n + 1)
                    pe.wait_ge(ready["wh"], n + 1)
                    o = per_batch(fill(step, h, t))
                    for b in range(BH):
                        i = mm(o[:, b, :], PT[:, h, b, :], wh[:, h, b, :], start=True, stop=True)
                    i.then_inc(full(step, h), 1)
                if step == "agg":
                    pe.wait_ge(ready["x3"], n + 1)
                    o = per_batch(fill(step, h, t))
                    for b in range(BH):
                        i = mm(o[:, b, :], x3[:, h, b, :], AHT[:], start=True, stop=True)
                    i.then_inc(full(step, h), 1)
                if step == "stat":
                    pe.wait_ge(ready["agg"], n + 1)
                    for k in range(2):
                        mm(fill(step, h, t, k), w1T_l3[:, k * 128:(k + 1) * 128], AGG[:, n, :],
                           start=True, stop=True).then_inc(full(step, h, k), 1)

            def lstm_gates(s, t):
                p, step, b0, nb = SLOTS[s]
                nw = N // p
                width = nb * nw
                unit = t - LAG["gates"]
                if p == 1:
                    pe.wait_ge(ready["xl"], unit * 2 + b0 // BH + 1)
                    src = xl[:, b0:b0 + nb, :]
                else:
                    src = HT[:, :, step:step + (nw - 1) * p + 1:p]
                wait(pe, h_ready, unit * NSLOT + s)
                for g in slot_gates(s):
                    o = G[:, g, 0:width].rearrange("p (b w) -> p b w", b=nb)
                    i = mm(o, wih[:, p - 1, g * D:(g + 1) * D], src, start=True, stop=(step == 0))
                    if step:
                        i = mm(o, whh[:, p - 1, g * D:(g + 1) * D],
                               hs[:, 0:width].rearrange("p (b w) -> p b w", b=nb), start=False, stop=True)
                    i.then_inc(gates_filled, 1)

            def body(t):
                for step, h in ORDER:
                    if present(step, t):
                        fused_step(step, h, t)

            bodies(pe, body)

            def hpre(g, par):
                for k in range(2):
                    wait(pe, relu_ready, (g - 2) * 2 + k + 1 if not isinstance(g, int) or g >= 2 else 0)
                    mm(G[:, 2 * par + k, :], w1T_l3[:, k * 128:(k + 1) * 128], AGG[:, g, :],
                       start=True, stop=True).then_inc(hpre_filled, 1)

            def features(g, par):
                wait(pe, out_kept, g - 1 if not isinstance(g, int) or g >= 2 else 0)
                for k in range(2):
                    pe.wait_ge(relu_ready, g * 2 + k + 1)
                    i = mm(F[:, par, :], w2T_l3[:, k, :], relu[:, par, k, :], start=(k == 0), stop=(k == 1))
                i.then_inc(out_filled, 1)

            pe.wait_ge(ready["stat"], 4 * UNITS)
            hpre(0, 0)
            hpre(1, 1)
            features(0, 0)
            with pe.Fori(2, GROUPS - 1, 2) as g:
                hpre(g, 0)
                features(g - 1, 1)
                hpre(g + 1, 1)
                features(g, 0)
            features(GROUPS - 1, 1)

            def rows(g, par):
                pe.wait_ge(affine_ready, g + 1)
                wait(pe, res_ready, g - 1 if not isinstance(g, int) or g >= 2 else 0)
                o = per_batch(F[:, 2 + par, :])
                for b in range(BH):
                    i = pe.transpose(o[:, b, :], oaff[:, par, b * N:(b + 1) * N], I_[:])
                i.then_inc(rows_filled, 1)

            rows(0, 0)
            rows(1, 1)
            with pe.Fori(2, GROUPS - 1, 2) as g:
                rows(g, 0)
                rows(g + 1, 1)

        @block.scalar
        def _(act):
            def dst_size(dst):
                n = 1
                for k in dst.shape[1:]:
                    n *= k
                return n

            def move(step, h, t, dst, name, func=ACT.Copy, j=0):
                wait_filled(act, step, h, t, j)
                src = bank_of(step, h, j)[:, 0:dst_size(dst)].rearrange("p (b n) -> p b n", b=dst.shape[1])
                act.activation(dst, src, func).then_inc(ready[name], 1)

            def fused_step(step, h, t):
                n = half_number(step, t, h) if step not in ("gates", "tanhc") else None
                if step == "ax":
                    move(step, h, t, yT[:, h], "yT")
                if step == "h1":
                    for j in range(2):
                        move(step, h, t, h1[:, h, 2 * j:2 * j + 2, :], f"h1_{j}", ACT.Relu, j)
                if step == "z":
                    move(step, h, t, z[:, h], "z")
                if step == "gax":
                    move(step, h, t, yT[:, h], "gyT")
                if step == "gh":
                    move(step, h, t, h1[:, h, :, 0:D], "gh1", ACT.Relu)
                if step == "gah":
                    move(step, h, t, y2T[:, h, 0], "gy2T")
                if step == "gx":
                    move(step, h, t, xl[:, BH * h:BH * h + BH, :], "xl", ACT.Relu)
                if step == "wh":
                    wait_filled(act, step, h, t, 1)
                    act.activation(s1[:, h], bank_of(step, h, 1)[:, 0:BH], ACT.Copy).then_inc(ready["s1"], 1)
                if step == "expo":
                    act.wait_ge(ready["nmax"], n + 1)
                    for b in range(BH):
                        i = act.activation(P[:, h, b, :], E[:, h, b, :], ACT.Exp, bias=nmax[:, h, b:b + 1],
                                           accum_out=psum_[:, h, b:b + 1])
                    i.then_inc(ready["P"], 1)
                if step == "gates":
                    p, _, _, nb = SLOTS[h]
                    width = nb * (N // p)
                    unit = t - LAG[step]
                    for i, g in enumerate(slot_gates(h)):
                        act.wait_ge(gates_filled, unit * GATES_BEFORE[NSLOT] + GATES_BEFORE[h] + i + 1)
                        act.activation(gact[:, g, 0:width], G[:, g, 0:width], ACT.Tanh,
                                       bias=gbias[:, p - 1, g:g + 1], scale=1.0 if g == GATE_G else 0.5)\
                            .then_inc(gates_done, 1)
                if step == "tanhc":
                    p, _, _, nb = SLOTS[h]
                    width = nb * (N // p)
                    act.wait_ge(cell_ready, (t - LAG[step]) * NSLOT + h + 1)
                    act.activation(tanhc[:, 0:width], cell[:, 0:width], ACT.Tanh, scale=0.5)\
                        .then_inc(tanhc_ready, 1)

            def body(t):
                for step, h in ORDER:
                    if present(step, t):
                        fused_step(step, h, t)

            act.wait_ge(setup_dve, SETUP_STEPS)
            bodies(act, body)

            act.wait_ge(bn_dve, 6)
            for h in range(2):
                act.wait_ge(x3_stored[h], 16 * UNITS)

            def relu_group(g, par):
                for k in range(2):
                    act.wait_ge(hpre_filled, g * 2 + k + 1)
                    wait(act, out_filled, g - 1 if not isinstance(g, int) or g >= 2 else 0)
                    act.activation(relu[:, par, k, :], G[:, 2 * par + k, :], ACT.Relu, bias=bn[:, 6 + k:7 + k],
                                   scale=bn[:, 8 + k:9 + k]).then_inc(relu_ready, 1)

            relu_group(0, 0)
            relu_group(1, 1)
            with act.Fori(2, GROUPS - 1, 2) as g:
                relu_group(g, 0)
                relu_group(g + 1, 1)

            def affine_group(g, par):
                wait(act, rows_filled, g - 1 if not isinstance(g, int) or g >= 2 else 0)
                act.wait_ge(bn_dve, 13)
                act.activation(oaff[:, par, :], AGG[:, g, :], ACT.Identity, bias=bn[:, 14:15],
                               scale=bn[:, 13:14]).then_inc(affine_ready, 1)

            affine_group(0, 0)
            affine_group(1, 1)
            with act.Fori(2, GROUPS - 1, 2) as g:
                affine_group(g, 0)
                affine_group(g + 1, 1)

        @block.vector
        def _(dve):
            setup = [0]

            def chain(i):
                setup[0] += 1
                i.then_inc(setup_dve, 1)
                dve.wait_ge(setup_dve, setup[0])

            dve.wait_ge(loaded, NLOAD)
            dve.wait_ge(setup_pool, 3)
            chain(V.tensor_scalar(maskadd[:], A_[:], 0.0, MASKED, ALU.is_equal, ALU.mult))
            chain(V.tensor_tensor(A2T[:], AT[:], AT[:], ALU.mult))
            chain(V.tensor_tensor(A_[:], A_[:], I_[:], ALU.add))
            chain(V.tensor_tensor(ANT[:], AT[:], I_[:], ALU.add))
            chain(V.tensor_tensor(scratch[:], A_[:], I_[:], ALU.mult))
            for k, m in enumerate((ANT, A_, scratch)):
                i = V.tensor_reduce(deg[:, k:k + 1], m[:], axis=AX.X, op=ALU.add)
            chain(i)
            V.tensor_tensor(deg[:, 3:4], deg[:, 0:1], deg[:, 1:2], ALU.add).then_inc(deg_sum, 1)
            dve.wait_ge(deg_sum, 1)
            chain(V.tensor_tensor(deg[:, 3:4], deg[:, 3:4], deg[:, 2:3], ALU.subtract))
            dve.wait_ge(setup_pool, 4)
            chain(V.tensor_scalar(scratch[:], I_[:], dinv[:], None, ALU.mult))
            chain(V.tensor_scalar(AHT[:], ANT[:], dinv[:], None, ALU.mult))
            dve.wait_ge(setup_pe, 4)
            chain(V.tensor_tensor(AHT[:], F[:, 3, 0:N], AHT[:], ALU.mult))
            for b in range(BH):
                i = V.tensor_copy(rs[:, b, :], F[0:1, 0, 0:N])
            chain(i)
            chain(V.tensor_copy(wa1[:], F[:, 1, 0:1]))
            chain(V.tensor_copy(wa2[:], F[:, 2, 0:128]))
            chain(V.tensor_scalar(wih[:, 1:SKIPS, :], wih[:, 1:SKIPS, :], 0.5, None, ALU.mult))
            chain(V.tensor_scalar(whh[:], whh[:], 0.5, None, ALU.mult))
            chain(V.tensor_tensor(gbias[:], gbias[:], bhh[:], ALU.add))
            for g in (GATE_I, GATE_F, GATE_O):
                chain(V.tensor_scalar(gbias[:, :, g], gbias[:, :, g], 0.5, None, ALU.mult))

            def take(step, h, t, dst, name, j=0, relu_=False):
                wait_filled(dve, step, h, t, j)
                src = per_batch(bank_of(step, h, j))
                if relu_:
                    i = V.tensor_scalar(dst, src, 0.0, None, ALU.max)
                else:
                    i = V.tensor_copy(dst, src)
                i.then_inc(ready[name], 1)

            def stats(n, h, r, count):
                dve.wait_ge(added[n], count)
                for b in range(BH):
                    i = V.bn_stats(lnst[:, n, h, b, :], r[:, b, :])
                i.then_inc(stated[n], 1)
                dve.wait_ge(stated[n], count)
                V.tensor_copy(carry[:], lnst[:, n, h, 0, 0:1])
                for b in range(BH):
                    i = V.bn_aggr(lnmv[:, n, h, b, :], lnst[:, n, h, b, :])
                i.then_inc(aggregated[n], 1)

            def normalise(n, h, r, name, count):
                dve.wait_ge(rstd[n], count)
                for b in range(BH):
                    i = V.tensor_scalar(r[:, b, :], r[:, b, :], lnmv[:, n, h, b, 0:1], lnr[:, n, h, b:b + 1],
                                        ALU.subtract, ALU.mult)
                i.then_inc(ready[name], 1)

            def fused_step(step, h, t):
                lstm = step in ("gates", "tanhc", "hout")
                n = None if lstm else half_number(step, t, h)
                if step == "ah1":
                    for k in range(2):
                        take(step, h, t, y2T[:, h, k], f"y2T_{k}", k)
                if step in ("h2a", "h2b"):
                    for j in range(2):
                        c = j + 2 * (step == "h2b")
                        if c == 0:
                            pass
                        take(step, h, t, h2T[:, c], f"h2T_{c}", j, True)
                if step == "oz":
                    if not isinstance(t, int) or t > 0:
                        dve.wait_ge(ready["x1_kept"], n - 1)
                    wait_filled(dve, step, h, t)
                    V.tensor_tensor(x1[:, h], per_batch(bank_of(step, h)), xin[:, h], ALU.add)\
                        .then_inc(added[0], 1)
                    stats(0, h, x1[:, h], n + 1)
                if step == "norm1":
                    normalise(0, h, x1[:, h], "x1", n + 1)
                if step == "backT":
                    wait_filled(dve, step, h, t)
                    dve.wait_ge(ready["x1_kept"], n + 1)
                    V.scalar_tensor_tensor(x2[:, h].rearrange("p b d -> p (b d)"), bank_of(step, h), 0.5,
                                           AGG[:, n, :], ALU.mult, ALU.add).then_inc(added[1], 1)
                    stats(1, h, x2[:, h], n + 1)
                if step == "norm2":
                    normalise(1, h, x2[:, h], "x2", n + 1)
                if step == "x2T":
                    take(step, h, t, x2T[:, h], "x2T")
                if step == "wh":
                    take(step, h, t, wh[:, h], "wh")
                if step == "s2":
                    wait_filled(dve, step, h, t)
                    dve.wait_ge(ready["s1"], n + 1)
                    o = per_batch(bank_of(step, h))
                    for b in range(BH):
                        i = V.scalar_tensor_tensor(E[:, h, b, :], o[:, b, :], s1[:, h, b:b + 1], maskadd[:],
                                                   ALU.add, ALU.add)
                    i.then_inc(ready["E"], 1)
                if step == "lrelu":
                    dve.wait_ge(ready["E"], n + 1)
                    V.scalar_tensor_tensor(E[:, h], E[:, h], ALPHA, E[:, h], ALU.mult, ALU.max)\
                        .then_inc(ready["L"], 1)
                if step == "rowmax":
                    dve.wait_ge(ready["L"], n + 1)
                    V.tensor_reduce(nmax[:, h], E[:, h], axis=AX.X, op=ALU.max, negate=True)\
                        .then_inc(ready["nmax"], 1)
                if step == "pT":
                    take(step, h, t, PT[:, h], "PT")
                    dve.wait_ge(ready["P"], n + 1)
                    V.reciprocal(rsum[:, h], psum_[:, h]).then_inc(ready["rsum"], 1)
                if step == "att":
                    wait_filled(dve, step, h, t)
                    dve.wait_ge(ready["rsum"], n + 1)
                    if not isinstance(t, int) or t > LAG[step]:
                        dve.wait_ge(x3_stored[h], (t - LAG[step]) * 16)
                    o = per_batch(bank_of(step, h))
                    for b in range(BH):
                        i = V.scalar_tensor_tensor(x3[:, h, b, :], o[:, b, :], rsum[:, h, b:b + 1],
                                                   x2[:, h, b, :], ALU.mult, ALU.add)
                    i.then_inc(added[2], 1)
                    stats(2, h, x3[:, h], n + 1)
                if step == "norm3":
                    normalise(2, h, x3[:, h], "x3", n + 1)
                if step == "agg":
                    wait_filled(dve, step, h, t)
                    V.tensor_scalar(AGG[:, n, :], bank_of(step, h), 1.0, None, ALU.mult).then_inc(ready["agg"], 1)
                if step == "stat":
                    for k in range(2):
                        dve.wait_ge(setup_dve, SETUP_STEPS)
                        wait_filled(dve, step, h, t, k)
                        V.bn_stats(stats1[:, k, n, :], bank_of(step, h, k)).then_inc(ready["stat"], 1)
                if step == "gates":
                    p, later, _, nb = SLOTS[h]
                    w = nb * (N // p)
                    unit = t - LAG[step]
                    done = unit * GATES_BEFORE[NSLOT] + GATES_BEFORE[h]
                    dve.wait_ge(gates_done, done + 2)
                    if not later:
                        V.scalar_tensor_tensor(cell[:, 0:w], gact[:, GATE_I, 0:w], 1.0, gact[:, GATE_G, 0:w],
                                               ALU.add, ALU.mult).then_inc(cell_ready, 1)
                    else:
                        V.scalar_tensor_tensor(iterm[:, 0:w], gact[:, GATE_I, 0:w], 1.0, gact[:, GATE_G, 0:w],
                                               ALU.add, ALU.mult).then_inc(terms_done, 1)
                        dve.wait_ge(gates_done, done + 3)
                        V.scalar_tensor_tensor(fterm[:, 0:w], gact[:, GATE_F, 0:w], 1.0, cell[:, 0:w],
                                               ALU.add, ALU.mult).then_inc(terms_done, 1)
                        dve.wait_ge(terms_done, unit * 2 * LATER_BEFORE[NSLOT] + 2 * LATER_BEFORE[h] + 2)
                        V.scalar_tensor_tensor(cell[:, 0:w], fterm[:, 0:w], 0.5, iterm[:, 0:w],
                                               ALU.mult, ALU.add).then_inc(cell_ready, 1)
                if step == "hout":
                    p, later, b0, nb = SLOTS[h]
                    nw = N // p
                    w = nb * nw
                    unit = t - LAG[step]
                    if later == p - 1:
                        dst = HT[:, b0:b0 + nb, p - 1:nw * p:p]
                    else:
                        dst = hs[:, 0:w].rearrange("p (b w) -> p b w", b=nb)
                    dve.wait_ge(tanhc_ready, unit * NSLOT + h + 1)
                    V.scalar_tensor_tensor(dst, gact[:, GATE_O, 0:w].rearrange("p (b w) -> p b w", b=nb), 1.0,
                                           tanhc[:, 0:w].rearrange("p (b w) -> p b w", b=nb),
                                           ALU.add, ALU.mult).then_inc(h_ready, 1)

            def body(t):
                for step, h in ORDER:
                    if present(step, t):
                        fused_step(step, h, t)

            bodies(dve, body)

            bns = [0]

            def bn_chain(i):
                bns[0] += 1
                i.then_inc(bn_dve, 1)
                dve.wait_ge(bn_dve, bns[0])

            dve.wait_ge(ready["stat"], 4 * UNITS)
            mv = scratch[:, 0:4].rearrange("p (k c) -> p k c", k=2)
            for k in range(2):
                i = V.bn_aggr(mv[:, k, :], stats1[:, k].rearrange("p g s -> p (g s)"))
            bn_chain(i)
            bn_chain(V.tensor_tensor(bn[:, 0:2], mv[:, :, 0], vec1[:, 0, :], ALU.add))
            bn_chain(V.tensor_scalar(bn[:, 2:4], mv[:, :, 1], EPS, None, ALU.add))
            dve.wait_ge(bn_pool, 1)
            bn_chain(V.tensor_tensor(bn[:, 8:10], bn[:, 4:6], vec1[:, 1, :], ALU.mult))
            bn_chain(V.tensor_tensor(bn[:, 0:2], vec1[:, 0, :], bn[:, 0:2], ALU.subtract))
            V.tensor_tensor(bn[:, 0:2], bn[:, 0:2], bn[:, 8:10], ALU.mult).then_inc(shift_term, 1)
            dve.wait_ge(shift_term, 1)
            bn_chain(V.tensor_tensor(bn[:, 6:8], bn[:, 0:2], vec1[:, 2, :], ALU.add))

            def keep(g, par):
                dve.wait_ge(setup_dve, SETUP_STEPS)
                dve.wait_ge(out_filled, g + 1)
                V.bn_stats(stats2[:, g, :], F[:, par, :]).then_inc(f_stats, 1)
                V.tensor_scalar(AGG[:, g, :], F[:, par, :], 1.0, None, ALU.mult).then_inc(out_kept, 1)

            with dve.Fori(0, GROUPS - 1, 2) as g:
                keep(g, 0)
                keep(g + 1, 1)

            dve.wait_ge(f_stats, GROUPS)
            bn_chain(V.bn_aggr(scratch[:, 8:10], stats2[:].rearrange("p g s -> p (g s)")))
            bn_chain(V.tensor_tensor(bn[:, 10:11], scratch[:, 8:9], vec2[:, 0, :], ALU.add))
            bn_chain(V.tensor_tensor(bn[:, 10:11], vec2[:, 0, :], bn[:, 10:11], ALU.subtract))
            bn_chain(V.tensor_scalar(bn[:, 11:12], scratch[:, 9:10], EPS, None, ALU.add))
            dve.wait_ge(bn_pool, 2)
            bn_chain(V.tensor_tensor(bn[:, 13:14], bn[:, 12:13], vec2[:, 1, :], ALU.mult))
            bn_chain(V.tensor_tensor(bn[:, 10:11], bn[:, 10:11], bn[:, 13:14], ALU.mult))
            bn_chain(V.tensor_tensor(bn[:, 14:15], bn[:, 10:11], vec2[:, 2, :], ALU.add))

            def residual(g, par):
                dve.wait_ge(rows_filled, g + 1)
                wait(dve, fin_ready, g - 1 if not isinstance(g, int) or g >= 2 else 0)
                V.tensor_tensor(res[:, par].rearrange("p b d -> p (b d)"), F[:, 2 + par, :],
                                X3[:, g, :], ALU.add).then_inc(res_ready, 1)
                dve.wait_ge(res_ready, g + 1)
                for b in range(BH):
                    i = V.bn_stats(lnst[:, 0, par, b, :], res[:, par, b, :])
                i.then_inc(f_stats, 1)
                dve.wait_ge(f_stats, g + 1 + GROUPS)
                V.tensor_copy(carry[:], lnst[:, 0, par, 0, 0:1])
                for b in range(BH):
                    i = V.bn_aggr(lnmv[:, 0, par, b, :], lnst[:, 0, par, b, :])
                i.then_inc(f_mv, 1)

            def finish(g, par):
                dve.wait_ge(f_rstd, g + 1)
                if not isinstance(g, int) or g >= 2:
                    dve.wait_ge(stored[par], (g - par) * 8)
                for b in range(BH):
                    i = V.tensor_scalar(fin[:, par, b, :], res[:, par, b, :], lnmv[:, 0, par, b, 0:1],
                                        lnr[:, 0, par, b:b + 1], ALU.subtract, ALU.mult)
                i.then_inc(fin_ready, 1)

            for h in range(2):
                dve.wait_ge(x3_stored[h], 16 * UNITS)
            dve.wait_ge(x3_back, 16 * 8)
            residual(0, 0)
            residual(1, 1)
            finish(0, 0)
            residual(2, 0)
            finish(1, 1)
            with dve.Fori(3, GROUPS - 1, 2) as g:
                residual(g, 1)
                finish(g - 1, 0)
                residual(g + 1, 0)
                finish(g, 1)
            residual(GROUPS - 1, 1)
            finish(GROUPS - 2, 0)
            finish(GROUPS - 1, 1)


def kernel(**inputs):
    import numpy as np
    import concourse.bacc as bacc
    from concourse import mybir as mb
    from concourse.bass_utils import run_bass_kernel_spmd as run

    i = {k: np.asarray(v) for k, v in inputs.items()}
    cols = lambda a, k: a.reshape(k, 128).T
    data = {
        "x": i["x"].reshape(GROUPS, BH, N, D).transpose(0, 2, 1, 3).reshape(GROUPS, N, BH, D),
        "adj": i["adj"], "adjT": i["adj"].T,
        "l0_w1": i["L0_gnn_W1"],
        "l0_w2": i["L0_gnn_W2"].reshape(2, 128, HID2).transpose(1, 0, 2),
        "l0_w3": i["L0_gnn_W3"].reshape(4, 128, D).transpose(1, 0, 2),
        "l1_wg0": i["L1_gnn_Wg0"], "l1_bg0": i["L1_gnn_bg0"].reshape(1, D),
        "l1_wg1": i["L1_gnn_Wg1"], "l1_bg1": i["L1_gnn_bg1"].reshape(1, D),
        "l1_wihT": i["L1_gnn_Wih"].transpose(2, 0, 1), "l1_whhT": i["L1_gnn_Whh"].transpose(2, 0, 1),
        "l1_bih": i["L1_gnn_bih"].reshape(SKIPS, 4, D).transpose(2, 0, 1),
        "l1_bhh": i["L1_gnn_bhh"].reshape(SKIPS, 4, D).transpose(2, 0, 1),
        "l2_w": i["L2_gnn_W"], "l2_wT": i["L2_gnn_W"].T, "l2_a": cols(i["L2_gnn_a"], 2),
        "l3_w1T": i["L3_gnn_W1"].T,
        "l3_vec1": np.stack([cols(i[f"L3_gnn_{n}"], 2) for n in ("b1", "g1", "be1")], 1),
        "l3_w2T": i["L3_gnn_W2"].T.reshape(2, 128, D).transpose(1, 0, 2),
        "l3_vec2": np.stack([cols(i[f"L3_gnn_{n}"], 1) for n in ("b2", "g2", "be2")], 1),
        "eye": np.eye(128, dtype=np.float32),
    }
    nc = bacc.Bacc("TRN2", target_bir_lowering=False, num_devices=1)
    arrays, args = {}, []
    for name, a in data.items():
        a = np.ascontiguousarray(a)
        arrays[f"in_{name}"] = a
        args.append(nc.dram_tensor(f"in_{name}", a.shape, mb.dt.from_np(a.dtype), kind="ExternalInput").ap())
    out = nc.dram_tensor("out_rows", (GROUPS, N, BH, D), mb.dt.float32, kind="ExternalOutput").ap()
    build_adj_resnorm_d4(nc, *args, out)
    r = run(nc, [arrays], core_ids=[0])
    o = r.results[0]["out_rows"]
    return o.transpose(0, 2, 1, 3).reshape(B, N, D)
```

```python
import concourse.bass as bass
from concourse import mybir
from contextlib import ExitStack

B, N, D = 128, 128, 128
BH = 4
COLS = BH * N
UB = 2 * BH
UNITS = B // UB
GROUPS = B // BH
HID1, HID2 = 256, 512
SKIPS = 4
RING = 4
PEEL = 8
EPS = 1e-5
ALPHA = 0.2
MASKED = -1.0e30
GATE_I, GATE_F, GATE_G, GATE_O = range(4)

SLOTS = [(1, 0, 0, BH), (1, 0, BH, BH)] + [(p, s, 0, UB) for p in range(2, SKIPS + 1) for s in range(p)]
NSLOT = len(SLOTS)


def slot_gates(s):
    return [GATE_I, GATE_G, GATE_O] if SLOTS[s][1] == 0 else [GATE_I, GATE_G, GATE_F, GATE_O]


GATES_BEFORE = [sum(len(slot_gates(k)) for k in range(s)) for s in range(NSLOT + 1)]
LATER_BEFORE = [sum(SLOTS[k][1] > 0 for k in range(s)) for s in range(NSLOT + 1)]

ORDER = [
    ("backT", 0), ("backT", 1), ("stats2", 0),
    ("gates", 0), ("tanhc", 0), ("ax", 0), ("ax", 1), ("stats2", 1), ("hout", 0), ("h1", 0), ("norm2", 0),
    ("gates", 1), ("tanhc", 1), ("norm2", 1), ("hout", 1), ("x2T", 0), ("x2T", 1), ("h1", 1), ("ah1", 0),
    ("gates", 2), ("tanhc", 2), ("hout", 2), ("wh", 0), ("wh", 1), ("s1", 0), ("s2", 0), ("lrelu", 0), ("s2", 1), ("rowmax", 0), ("lrelu", 1), ("rowmax", 1),
    ("gates", 3), ("tanhc", 3), ("hout", 3), ("expo", 0), ("h2a", 0), ("expo", 1), ("h2b", 0),
    ("gates", 4), ("tanhc", 4), ("hout", 4), ("ah1", 1), ("z", 0),
    ("gates", 5), ("tanhc", 5), ("hout", 5), ("pT", 0), ("pT", 1), ("h2a", 1), ("att", 0),
    ("gates", 6), ("tanhc", 6), ("hout", 6), ("att", 1), ("stats3", 0), ("h2b", 1), ("oz", 0), ("stats3", 1), ("norm3", 0),
    ("gates", 7), ("tanhc", 7), ("hout", 7), ("stats1", 0), ("norm3", 1), ("z", 1), ("norm1", 0),
    ("gates", 8), ("tanhc", 8), ("hout", 8), ("agg", 0), ("agg", 1), ("oz", 1), ("gax", 0), ("stats1", 1),
    ("gates", 9), ("tanhc", 9), ("hout", 9), ("stat", 0), ("norm1", 1), ("stat", 1),
    ("gates", 10), ("tanhc", 10), ("hout", 10), ("gh", 0), ("gax", 1), ("gah", 0), ("gh", 1), ("gx", 0), ("gah", 1), ("gx", 1),
]
FILLS = {"ax": 1, "h1": 2, "ah1": 2, "h2a": 2, "h2b": 2, "z": 1, "oz": 1, "gax": 1, "gh": 1, "gah": 1, "gx": 1,
         "backT": 1, "x2T": 1, "wh": 1, "s2": 1, "pT": 1, "att": 1, "agg": 1, "stat": 2}
LAG = {s: 0 for s in ("ax", "stats1", "h1", "ah1", "h2a", "h2b", "z", "oz", "norm1", "gax", "gh", "gah", "gx")}
LAG |= {s: 1 for s in ("gates", "tanhc", "hout")}
LAG |= {s: 2 for s in ("backT", "s1", "stats2", "stats3", "norm2", "x2T", "wh", "s2", "lrelu", "rowmax", "expo", "pT", "att", "norm3",
                       "agg", "stat")}
NBANK = 4
SETUP_STEPS = 10
BODIES = UNITS + 2
LOOP0, LOOP1 = 3, UNITS


def active(step, t):
    return 0 <= t - LAG[step] < UNITS


FILL_LIST = [(s, h, j) for s, h in ORDER if s in FILLS for j in range(FILLS[s])]
BANK = {f: i % NBANK for i, f in enumerate(FILL_LIST)}
PER_BODY = [sum(BANK[f] == k for f in FILL_LIST) for k in range(NBANK)]


def fills_in(t, bank, upto=None):
    n = 0
    for f in FILL_LIST:
        if f == upto:
            break
        n += BANK[f] == bank and active(f[0], t)
    return n


def fill_number(f, t):
    bank = BANK[f]
    if isinstance(t, int):
        return sum(fills_in(q, bank) for q in range(t)) + fills_in(t, bank, f) + 1
    base = sum(fills_in(q, bank) for q in range(LOOP0)) + fills_in(LOOP0, bank, f) + 1
    return (t - LOOP0) * PER_BODY[bank] + base


def fill_before(f, t):
    q, at = (t, t) if isinstance(t, int) else (LOOP0, t)
    while q >= 0:
        here = [e for e in FILL_LIST if BANK[e] == BANK[f] and active(e[0], q)]
        if f in here and at is t:
            here = here[:here.index(f)]
        if here:
            return here[-1], at
        q, at = q - 1, at - 1
    return None


def build_adj_resnorm_d4(nc, x, adj, adjT, l0_w1, l0_w2, l0_w3, l1_wg0, l1_bg0, l1_wg1, l1_bg1, l1_wihT, l1_whhT,
                         l1_bih, l1_bhh, l2_w, l2_wT, l2_a, l3_w1T, l3_vec1, l3_w2T, l3_vec2, eye, out):
    fp32 = mybir.dt.float32
    fp32r = mybir.dt.float32r
    HI, LO = 0, 1
    PASSES = ((HI, HI), (LO, HI), (HI, LO))
    ALU = mybir.AluOpType
    ACT = mybir.ActivationFunctionType
    AX = mybir.AxisListType
    V = nc.vector

    ctx = ExitStack()
    with ctx:
        def sb(name, shape, dt=fp32, where=ctx):
            return where.enter_context(nc.sbuf_tensor(name, shape, dt))

        def sem(name):
            return ctx.enter_context(nc.semaphore(name))

        A_ = sb("A_", [128, N])
        AT = sb("AT", [128, N])
        ANT = sb("ANT", [128, N])
        A2T = sb("A2T", [128, N])
        AHT = sb("AHT", [128, N])
        I_ = sb("I_", [128, 128])
        I_r = sb("I_r", [128, 128], fp32r)
        maskadd = sb("maskadd", [128, N])
        w1 = sb("w1", [128, HID1])
        w2 = sb("w2", [128, 2, 2, HID2], fp32r)
        w3 = sb("w3", [128, 4, D])
        wg0 = sb("wg0", [128, D])
        wg1 = sb("wg1", [128, D])
        bg = sb("bg", [1, 2, D])
        bg_hl = sb("bg_hl", [1, 2, 2, D], fp32r)
        rs = sb("rs", [1, N])
        rs_hl = sb("rs_hl", [1, 2, N], fp32r)
        rs4 = sb("rs4", [4, 1, N], fp32r)
        bg4 = sb("bg4", [4, 2, D], fp32r)
        wih = sb("wih", [128, 2, SKIPS, 4 * D], fp32r)
        whh = sb("whh", [128, 2, SKIPS - 1, 4 * D], fp32r)
        gbias = sb("gbias", [128, SKIPS, 4])
        bhh = sb("bhh", [128, SKIPS, 4])
        w_l2 = sb("w_l2", [128, D])
        w_l2T = sb("w_l2T", [128, D])
        a12 = sb("a12", [128, 2])
        wa1 = sb("wa1", [128, 1])
        wa2 = sb("wa2", [128, 128])
        w1T_l3 = sb("w1T_l3", [128, HID1])
        w2T_l3 = sb("w2T_l3", [128, 2, D])
        vec1 = sb("vec1", [128, 3, 2])
        vec2 = sb("vec2", [128, 3, 1])
        ones = sb("ones", [128, 128])
        scratch = sb("scratch", [128, 128])
        deg = sb("deg", [128, 4])
        dinv = sb("dinv", [128, 1])
        eps4 = sb("eps4", [128, BH])
        mhalf = sb("mhalf", [128, BH])
        AGG = sb("AGG", [128, GROUPS, COLS])
        stats1 = sb("stats1", [128, 2, GROUPS, 6])
        stats2 = sb("stats2", [128, GROUPS, 6])
        bn = sb("bn", [128, 16])
        fst = sb("fst", [128, RING, BH, 6])
        fmv = sb("fmv", [128, RING, BH, 2])
        fve = sb("fve", [128, RING, BH])
        frs = sb("frs", [128, RING, BH])
        fnm = sb("fnm", [128, RING, BH])
        fnb = sb("fnb", [128, RING, BH])
        mone = sb("mone", [128, BH])
        lnst = sb("lnst", [128, 3, 2, BH, 6])
        lnmv = sb("lnmv", [128, 3, 2, BH, 2])
        lnve = sb("lnve", [128, 3, 2, BH])
        lnr = sb("lnr", [128, 3, 2, BH])
        carry = sb("carry", [128, 1])
        s1 = sb("s1", [128, UB])
        nmax = sb("nmax", [128, 2, BH])
        psum_ = sb("psum_", [128, 2, BH])
        rsum = sb("rsum", [128, 2, BH])

        fused = ExitStack()
        with fused:
            def fb(name, shape):
                return sb(name, shape, fp32, fused)

            def fr(name, shape):
                return sb(name, shape, fp32r, fused)

            xin = fb("xin", [128, 2, BH, D])
            yT = fb("yT", [128, 2, BH, N])
            h1 = fb("h1", [128, 2, BH, HID1])
            y2T = fr("y2T", [128, 2, 2, BH, N])
            h2T = fb("h2T", [128, 4, BH, N])
            z = fb("z", [128, 2, BH, D])
            x1 = fb("x1", [128, 2, BH, D])
            xl = fr("xl", [128, 2, UB, N])
            x2 = fb("x2", [128, 2, BH, D])
            x2T = fb("x2T", [128, 2, BH, N])
            wh = fb("wh", [128, 2, BH, D])
            E = fb("E", [128, 2, BH, N])
            gact = fb("gact", [128, COLS])
            cell = fb("cell", [128, COLS])
            tanhc = fb("tanhc", [128, COLS])
            hnew = fb("hnew", [128, COLS])
            hs = fr("hs", [128, 2, COLS])
            HT = fr("HT", [128, 2, UB, N])
        X3 = sb("X3", [128, GROUPS, COLS])
        features_only = ExitStack()
        with features_only:
            relu = sb("relu", [128, RING, 2, COLS], fp32, features_only)
        oaff = sb("oaff", [128, 2, COLS])
        res = sb("res", [128, RING, BH, D])
        fin = sb("fin", [128, RING, BH, D])

        G = ctx.enter_context(nc.psum_tensor("G", [128, 4, COLS], fp32))
        F = ctx.enter_context(nc.psum_tensor("F", [128, NBANK, COLS], fp32))
        s1_bank = G[:, GATE_F, 0:UB]
        x3_dram = nc.dram_tensor("x3_dram", (GROUPS, 128, COLS), fp32, kind="Internal").ap()

        loaded_first = sem("adjacency_loaded")
        loaded = sem("weights_loaded")
        rows_built = sem("bias_rows_built")
        split_hi, split_lo = sem("weights_hi_ready"), sem("weights_lo_ready")
        eye_loaded = sem("eye_loaded")
        filled = [sem(f"bank{k}_filled") for k in range(NBANK)]
        x_loaded = [sem(f"x_half{h}_loaded") for h in range(2)]
        names = ["yT", "h1_0", "h1_1", "y2T_0", "y2T_1", "h2T_0", "h2T_1", "h2T_2", "h2T_3", "z", "r1", "x1",
                 "x1_kept", "gyT", "gh1", "gy2T", "xl", "r2", "x2", "x2T", "wh", "s1", "E", "L", "nmax", "P",
                 "rsum", "PT", "r3", "x3", "agg", "stat", "y2T_hi0", "y2T_hi1", "xl_hi"]
        ready = {n: sem(f"{n}_ready") for n in names}
        h2T_read = sem("h2T_read")
        added = [sem(f"ln{n}_added") for n in range(3)]
        stated = [sem(f"ln{n}_stats") for n in range(3)]
        aggregated = [sem(f"ln{n}_mean_var") for n in range(3)]
        eps_added = [sem(f"ln{n}_eps_added") for n in range(3)]
        rstd = [sem(f"ln{n}_rstd") for n in range(3)]
        s1_filled = sem("s1_filled")
        gates_filled = sem("gates_filled")
        gates_done = sem("gates_done")
        terms_done = sem("cell_terms_done")
        cell_ready = sem("cell_ready")
        tanhc_ready = sem("tanhc_ready")
        h_made = sem("lstm_h_made")
        h_hi = sem("lstm_h_hi_ready")
        h_ready = sem("lstm_h_lo_ready")
        x3_stored = [sem(f"x3_half{h}_stored") for h in range(2)]
        setup_dve = sem("setup_dve")
        setup_pe = sem("setup_pe")
        setup_pool = sem("setup_pool")
        setup_act = sem("setup_act")
        bn_dve = sem("bn_dve")
        shift_term = sem("shift_term")
        bias_ready = sem("lstm_bias_ready")
        bn_pool = sem("bn_pool")
        hpre_filled = sem("hpre_filled")
        relu_ready = sem("relu_ready")
        out_filled = sem("out_filled")
        out_kept = sem("out_kept")
        x3_back = sem("x3_back")
        affine_ready = sem("affine_ready")
        rows_filled = sem("rows_filled")
        res_ready = sem("residual_ready")
        f_stats, f_mv, f_eps, f_rstd = sem("fin_stats"), sem("fin_mean_var"), sem("fin_eps_added"), sem("fin_rstd")
        f_pow = sem("fin_pow")
        fin_ready = sem("fin_ready")
        stored = [sem(f"out_ring{r}_stored") for r in range(RING)]

        w2_raw = AGG[:, 0:2, :]
        wih_raw = AGG[:, 2:2 + SKIPS, :]
        whh_raw = AGG[:, 2 + SKIPS:1 + 2 * SKIPS, :]
        FIRST_LOADS = [(AT, adjT), (A_, adj), (I_, eye), (w_l2T, l2_wT), (a12, l2_a), (w1, l0_w1),
                       (bg[:, 0, :], l1_bg0), (bg[:, 1, :], l1_bg1)]
        LOADS = [(w2_raw, l0_w2), (w3, l0_w3), (wih_raw, l1_wihT), (whh_raw, l1_whhT[:, 1:SKIPS, :]),
                 (wg0, l1_wg0), (wg1, l1_wg1), (gbias, l1_bih), (bhh, l1_bhh), (w_l2, l2_w),
                 (w1T_l3, l3_w1T), (w2T_l3, l3_w2T), (vec1, l3_vec1), (vec2, l3_vec2)]
        SPLITS = [(w2_raw[:, k, :], w2[:, :, k, :], 1.0) for k in range(2)]
        SPLITS += [(wih_raw[:, p, :], wih[:, :, p, :], 0.5 if p else 1.0) for p in range(SKIPS)]
        SPLITS += [(whh_raw[:, p, :], whh[:, :, p, :], 0.5) for p in range(SKIPS - 1)]
        NFIRST, NLOAD = 16 * len(FIRST_LOADS), 16 * len(LOADS)

        def wait(eng, s, n):
            if not isinstance(n, int) or n > 0:
                eng.wait_ge(s, n)

        def bodies(eng, body):
            for t in range(LOOP0):
                body(t)
            with eng.Fori(LOOP0, LOOP1) as t:
                body(t)
            for t in range(LOOP1, BODIES):
                body(t)

        def ring(eng, one, until=GROUPS):
            for g in range(PEEL):
                one(g, g % RING)
            with eng.Fori(PEEL, GROUPS - RING + 1, RING) as g:
                for r in range(RING):
                    one(g + r, r)

        def late(g, n):
            return n if not isinstance(g, int) or g >= RING else 0

        def present(step, t):
            return not isinstance(t, int) or active(step, t)

        def half_number(step, t, h):
            return (t - LAG[step]) * 2 + h

        def bank_of(step, h, j=0):
            return F[:, BANK[(step, h, j)], :]

        def wait_filled(eng, step, h, t, j=0):
            f = (step, h, j)
            eng.wait_ge(filled[BANK[f]], fill_number(f, t))

        PRODUCT = {"ax": "yT", "z": "z", "gax": "gyT", "gh": "gh1", "gah": "gy2T", "gx": "xl", "x2T": "x2T",
                   "wh": "wh",
                   "s2": "E", "pT": "PT", "agg": "agg"}
        PRODUCTS = {"h1": ("h1_0", "h1_1"), "ah1": ("y2T_0", "y2T_1"), "h2a": ("h2T_0", "h2T_1"),
                    "h2b": ("h2T_2", "h2T_3")}
        SUMS = {"oz": 0, "backT": 1, "att": 2}

        def read_signal(f, t):
            step, h, j = f
            n = half_number(step, t, h)
            if step == "stat":
                return ready["stat"], 2 * n + j + 1
            if step == "z":
                return ready["z"], n + 1
            if step in SUMS:
                return added[SUMS[step]], n + 1
            return ready[PRODUCT[step] if step in PRODUCT else PRODUCTS[step][j]], n + 1

        def h_views(s):
            p, step, b0, nb = SLOTS[s]
            nw = N // p
            src = hnew[:, 0:nb * nw].rearrange("p (b w) -> p b w", b=nb)
            if step == p - 1:
                return src, [HT[:, d, b0:b0 + nb, p - 1:nw * p:p] for d in (HI, LO)]
            return src, [hs[:, d, 0:nb * nw].rearrange("p (b w) -> p b w", b=nb) for d in (HI, LO)]

        def per_batch(ap):
            return ap.rearrange("p (b n) -> p b n", b=BH)

        block = ctx.enter_context(nc.Block())

        @block.sync
        def _(sp):
            for h in range(2):
                sp.dma_start(xin[:, h], x[h]).then_inc(x_loaded[h], 16)
            for dst, src in FIRST_LOADS:
                sp.dma_start(dst[:] if dst.__class__ is not bass.AP else dst, src).then_inc(loaded_first, 16)
            for dst, src in LOADS:
                sp.dma_start(dst[:] if dst.__class__ is not bass.AP else dst, src).then_inc(loaded, 16)
            sp.wait_ge(setup_dve, SETUP_STEPS)
            for k in range(4):
                sp.dma_start(rs4[k:k + 1, 0, :].bitcast(fp32), rs_hl[:, k // 2, :].bitcast(fp32))\
                  .then_inc(rows_built, 16)
                sp.dma_start(bg4[k:k + 1, :, :].bitcast(fp32), bg_hl[:, :, k % 2, :].bitcast(fp32))\
                  .then_inc(rows_built, 16)

            def body(t):
                for step, h in ORDER:
                    if not present(step, t):
                        continue
                    if step == "oz" and (not isinstance(t, int) or t + 1 < UNITS):
                        sp.wait_ge(added[0], half_number(step, t, h) + 1)
                        sp.dma_start(xin[:, h], x[(t + 1) * 2 + h]).then_inc(x_loaded[h], 16)
                    if step == "norm3":
                        sp.wait_ge(ready["x3"], half_number(step, t, h) + 1)
                        sp.dma_start(x3_dram[half_number(step, t, h)],
                                     x2[:, h]).then_inc(x3_stored[h], 16)

            for t in range(LOOP0):
                body(t)
            with sp.Fori(LOOP0, LOOP1 - 1) as t:
                body(t)
            for t in range(LOOP1 - 1, BODIES):
                body(t)

            sp.wait_ge(ready["stat"], 4 * UNITS)
            for h in range(2):
                sp.wait_ge(x3_stored[h], 16 * UNITS)
            parts = 8
            q = GROUPS // parts
            for i in range(parts):
                sp.dma_start(X3[:, i * q:(i + 1) * q, :],
                             x3_dram[i * q:(i + 1) * q].rearrange("g p c -> p g c")).then_inc(x3_back, 16)

            def store(g, r):
                sp.wait_ge(fin_ready, g + 1)
                sp.dma_start(out[g], fin[:, r]).then_inc(stored[r], 16)

            ring(sp, store)
            for r in range(RING):
                sp.wait_ge(stored[r], 16 * (GROUPS // RING))

        @block.gpsimd
        def _(pool):
            pool.memset(eps4[:], EPS).then_inc(setup_pool, 1)
            pool.memset(mhalf[:], -0.5).then_inc(setup_pool, 1)
            pool.memset(ones[:], 1.0).then_inc(setup_pool, 1)
            pool.memset(mone[:], -1.0).then_inc(setup_pool, 1)
            pool.wait_ge(setup_pool, 4)
            pool.wait_ge(setup_dve, 6)
            pool.tensor_tensor(dinv[:], deg[:, 3:4], mhalf[:, 0:1], ALU.pow).then_inc(setup_pool, 1)

            def make_rstd(n, h, count):
                pool.wait_ge(aggregated[n], count)
                pool.tensor_tensor(lnve[:, n, h, :], lnmv[:, n, h, :, 1], eps4[:], ALU.add).then_inc(eps_added[n], 1)
                pool.wait_ge(eps_added[n], count)
                pool.tensor_tensor(lnr[:, n, h, :], lnve[:, n, h, :], mhalf[:], ALU.pow).then_inc(rstd[n], 1)

            def body(t):
                for step, h in ORDER:
                    if not present(step, t):
                        continue
                    if step == "stats1":
                        make_rstd(0, h, half_number(step, t, h) + 1)
                    if step == "stats2":
                        make_rstd(1, h, half_number(step, t, h) + 1)
                    if step == "stats3":
                        make_rstd(2, h, half_number(step, t, h) + 1)
                    if step == "norm1":
                        n = half_number(step, t, h)
                        if isinstance(t, int) and t == 0:
                            pool.wait_ge(split_hi, len(SPLITS))
                            pool.wait_ge(split_lo, len(SPLITS))
                        pool.wait_ge(setup_pool, 5)
                        pool.wait_ge(ready["x1"], n + 1)
                        pool.tensor_copy(AGG[:, n, :],
                                         x1[:, h].rearrange("p b d -> p (b d)")).then_inc(ready["x1_kept"], 1)

            bodies(pool, body)

            pool.wait_ge(bn_dve, 3)
            pool.tensor_tensor(bn[:, 4:6], bn[:, 2:4], mhalf[:, 0:2], ALU.pow).then_inc(bn_pool, 1)
            pool.wait_ge(bn_dve, 10)
            pool.tensor_tensor(bn[:, 12:13], bn[:, 11:12], mhalf[:, 0:1], ALU.pow).then_inc(bn_pool, 1)

            def fin_rstd(g, r):
                pool.wait_ge(f_mv, g + 1)
                pool.tensor_tensor(fve[:, r, :], fmv[:, r, :, 1], eps4[:], ALU.add)
                pool.tensor_tensor(fnm[:, r, :], fmv[:, r, :, 0], mone[:], ALU.mult).then_inc(f_eps, 1)
                pool.wait_ge(f_eps, g + 1)
                pool.tensor_tensor(frs[:, r, :], fve[:, r, :], mhalf[:], ALU.pow).then_inc(f_pow, 1)
                pool.wait_ge(f_pow, g + 1)
                pool.tensor_tensor(fnb[:, r, :], fnm[:, r, :], frs[:, r, :], ALU.mult).then_inc(f_rstd, 1)

            ring(pool, fin_rstd)

        @block.tensor
        def _(pe):
            mm = pe.matmul
            pe.wait_ge(loaded_first, NFIRST)
            pe.wait_ge(setup_pool, 4)
            mm(F[0:1, 0, 0:N], ones[:, 0:1], AT[:], start=True, stop=True).then_inc(setup_pe, 1)
            mm(F[:, 1, 0:1], w_l2T[:], a12[:, 0:1], start=True, stop=True).then_inc(setup_pe, 1)
            mm(F[:, 2, 0:128], w_l2T[:], a12[:, 1:2].to_broadcast([128, 128]),
               start=True, stop=True).then_inc(setup_pe, 1)
            pe.wait_ge(setup_dve, 7)
            mm(F[:, 3, 0:N], ones[:], scratch[:], start=True, stop=True).then_inc(setup_pe, 1)
            pe.wait_ge(setup_dve, SETUP_STEPS)

            def fill(step, h, t, j=0):
                f = (step, h, j)
                before = fill_before(f, t)
                if before:
                    pe.wait_ge(*read_signal(*before))
                return F[:, BANK[f], :]

            def full(step, h, j=0):
                return filled[BANK[(step, h, j)]]

            def fused_step(step, h, t):
                n = half_number(step, t, h) if step != "gates" else None
                if step == "ax":
                    pe.wait_ge(x_loaded[h], (t - LAG[step]) * 16 + 16)
                    o = per_batch(fill(step, h, t))
                    for b in range(BH):
                        i = mm(o[:, b, :], xin[:, h, b, :], A2T[:], start=True, stop=True)
                    i.then_inc(full(step, h), 1)
                if step == "h1":
                    pe.wait_ge(ready["yT"], n + 1)
                    for j in range(2):
                        o = fill(step, h, t, j).rearrange("p (b f) -> p b f", b=2)
                        for b in range(2):
                            i = mm(o[:, b, :], yT[:, h, 2 * j + b, :], w1[:], start=True, stop=True)
                        i.then_inc(full(step, h, j), 1)
                if step == "ah1":
                    pe.wait_ge(ready["h1_0"], n + 1)
                    pe.wait_ge(ready["h1_1"], n + 1)
                    for k in range(2):
                        o = per_batch(fill(step, h, t, k))
                        for b in range(BH):
                            i = mm(o[:, b, :], h1[:, h, b, k * 128:(k + 1) * 128], A2T[:], start=True, stop=True)
                        i.then_inc(full(step, h, k), 1)
                if step in ("h2a", "h2b"):
                    if isinstance(t, int) and t == 0:
                        pe.wait_ge(split_lo, 2)
                    for j in range(2):
                        c = j + 2 * (step == "h2b")
                        o = per_batch(fill(step, h, t, j))
                        for k in range(2):
                            if c == 0:
                                pe.wait_ge(ready[f"y2T_{k}"], n + 1)
                            for a, d in PASSES:
                                i = mm(o, w2[:, a, k, c * 128:(c + 1) * 128], y2T[:, d, k],
                                       start=(k == 0 and a == d), stop=(k == 1 and (a, d) == PASSES[-1]))
                        i.then_inc(full(step, h, j), 1)
                if step == "z":
                    o = per_batch(fill(step, h, t))
                    for c in range(4):
                        pe.wait_ge(ready[f"h2T_{c}"], n + 1)
                    for b in range(BH):
                        for c in range(4):
                            i = mm(o[:, b, :], h2T[:, c, b, :], w3[:, c, :], start=(c == 0), stop=(c == 3))
                    i.then_inc(full(step, h), 1)
                if step == "oz":
                    pe.wait_ge(ready["z"], n + 1)
                    mm(per_batch(fill(step, h, t)), A2T[:], z[:, h], start=True, stop=True)\
                        .then_inc(full(step, h), 1)
                if step == "gax":
                    pe.wait_ge(ready["x1"], n + 1)
                    o = per_batch(fill(step, h, t))
                    for b in range(BH):
                        i = mm(o[:, b, :], x1[:, h, b, :], AT[:], start=True, stop=True)
                    i.then_inc(full(step, h), 1)
                if step == "gh":
                    pe.wait_ge(ready["gyT"], n + 1)
                    o = per_batch(fill(step, h, t))
                    if isinstance(t, int) and t == 0:
                        pe.wait_ge(rows_built, 16 * 4 * 2)
                    mm(o, rs4[:, 0, :], bg4[:, 0:1, :].to_broadcast([4, BH, D]), start=True, stop=False, skip_group_check=True)
                    for b in range(BH):
                        i = mm(o[:, b, :], yT[:, h, b, :], wg0[:], start=False, stop=(b == BH - 1),
                               skip_group_check=True)
                    i.then_inc(full(step, h), 1)
                if step == "gah":
                    pe.wait_ge(ready["gh1"], n + 1)
                    o = per_batch(fill(step, h, t))
                    for b in range(BH):
                        i = mm(o[:, b, :], h1[:, h, b, 0:D], AT[:], start=True, stop=True)
                    i.then_inc(full(step, h), 1)
                if step == "gx":
                    pe.wait_ge(ready["gy2T"], n + 1)
                    o = per_batch(fill(step, h, t))
                    mm(o, bg4[:, 1, :], rs4[:].to_broadcast([4, BH, N]), start=True, stop=False)
                    mm(o, wg1[:], z[:, h], start=False, stop=True).then_inc(full(step, h), 1)
                if step == "gates":
                    lstm_gates(h, t)
                if step == "backT":
                    pe.wait_ge(h_ready, (t - LAG[step]) * NSLOT + NSLOT)
                    o = per_batch(fill(step, h, t))
                    for b in range(BH):
                        for d in (HI, LO):
                            i = mm(o[:, b, :], HT[:, d, BH * h + b, :], I_r[:], start=(d == HI), stop=(d == LO))
                    i.then_inc(full(step, h), 1)
                if step == "x2T":
                    pe.wait_ge(ready["x2"], n + 1)
                    o = per_batch(fill(step, h, t))
                    for b in range(BH):
                        i = pe.transpose(o[:, b, :], x2[:, h, b, :], I_[:])
                    i.then_inc(full(step, h), 1)
                if step == "wh":
                    pe.wait_ge(ready["x2T"], n + 1)
                    o = per_batch(fill(step, h, t))
                    for b in range(BH):
                        i = mm(o[:, b, :], x2T[:, h, b, :], w_l2[:], start=True, stop=True)
                    i.then_inc(full(step, h), 1)
                if step == "s1":
                    for b in range(UB):
                        i = mm(s1_bank[:, b:b + 1], x2T[:, b // BH, b % BH, :], wa1[:], start=True, stop=True)
                    i.then_inc(s1_filled, 1)
                if step == "s2":
                    mm(per_batch(fill(step, h, t)), wa2[:], x2T[:, h], start=True, stop=True)\
                        .then_inc(full(step, h), 1)
                if step == "pT":
                    pe.wait_ge(ready["P"], n + 1)
                    o = per_batch(fill(step, h, t))
                    for b in range(BH):
                        i = pe.transpose(o[:, b, :], E[:, h, b, :], I_[:])
                    i.then_inc(full(step, h), 1)
                if step == "att":
                    pe.wait_ge(ready["PT"], n + 1)
                    pe.wait_ge(ready["wh"], n + 1)
                    o = per_batch(fill(step, h, t))
                    for b in range(BH):
                        i = mm(o[:, b, :], x2T[:, h, b, :], wh[:, h, b, :], start=True, stop=True)
                    i.then_inc(full(step, h), 1)
                if step == "agg":
                    pe.wait_ge(ready["x3"], n + 1)
                    o = per_batch(fill(step, h, t))
                    for b in range(BH):
                        i = mm(o[:, b, :], x2[:, h, b, :], AHT[:], start=True, stop=True)
                    i.then_inc(full(step, h), 1)
                if step == "stat":
                    pe.wait_ge(ready["agg"], n + 1)
                    for k in range(2):
                        mm(fill(step, h, t, k), w1T_l3[:, k * 128:(k + 1) * 128], AGG[:, n, :],
                           start=True, stop=True).then_inc(full(step, h, k), 1)

            def lstm_gates(s, t):
                p, step, b0, nb = SLOTS[s]
                nw = N // p
                width = nb * nw
                unit = t - LAG["gates"]
                if isinstance(t, int) and unit == 0 and s == 0:
                    pe.wait_ge(split_lo, len(SPLITS))
                if p == 1:
                    pe.wait_ge(ready["xl"], unit * 2 + b0 // BH + 1)
                    src = [xl[:, d, b0:b0 + nb, :] for d in (HI, LO)]
                else:
                    src = [HT[:, d, :, step:step + (nw - 1) * p + 1:p] for d in (HI, LO)]
                    inner = [hs[:, d, 0:width].rearrange("p (b w) -> p b w", b=nb) for d in (HI, LO)]
                gates = slot_gates(s)
                out_of = {g: G[:, g, 0:width].rearrange("p (b w) -> p b w", b=nb) for g in gates}

                def column(w, a, g):
                    return w[:, a, p - 1, g * D:(g + 1) * D]

                wait(pe, h_made if s == 1 else h_ready, unit * NSLOT + s)
                if s == 3 and present("wh", t):
                    pe.wait_ge(ready["s1"], t - LAG["s1"] + 1)
                for g in gates:
                    for a, d in PASSES:
                        i = mm(out_of[g], column(wih, a, g), src[d], start=(a == d),
                               stop=(not step and (a, d) == PASSES[-1]))
                    if step:
                        for a, d in PASSES:
                            i = mm(out_of[g], whh[:, a, p - 2, g * D:(g + 1) * D], inner[d], start=False,
                                   stop=(a, d) == PASSES[-1])
                    i.then_inc(gates_filled, 1)

            def body(t):
                for step, h in ORDER:
                    if present(step, t):
                        fused_step(step, h, t)

            bodies(pe, body)

            def hpre(g, r):
                for k in range(2):
                    wait(pe, relu_ready, (g - 2) * 2 + k + 1 if not isinstance(g, int) or g >= 2 else 0)
                    mm(G[:, 2 * (r % 2) + k, :], w1T_l3[:, k * 128:(k + 1) * 128], AGG[:, g, :],
                       start=True, stop=True).then_inc(hpre_filled, 1)

            def features(g, r):
                wait(pe, out_kept, late(g, g - RING + 1))
                for k in range(2):
                    pe.wait_ge(relu_ready, g * 2 + k + 1)
                    i = mm(F[:, r, :], w2T_l3[:, k, :], relu[:, r, k, :], start=(k == 0), stop=(k == 1))
                i.then_inc(out_filled, 1)

            def one(g, r):
                hpre(g, r)
                if not isinstance(g, int) or g >= 2:
                    features(g - 2, (r - 2) % RING)

            pe.wait_ge(ready["stat"], 4 * UNITS)
            ring(pe, one)
            features(GROUPS - 2, RING - 2)
            features(GROUPS - 1, RING - 1)

            def rows(g, r):
                pe.wait_ge(affine_ready, g + 1)
                wait(pe, res_ready, late(g, g - RING + 1))
                o = per_batch(F[:, r, :])
                for b in range(BH):
                    i = pe.transpose(o[:, b, :], oaff[:, r % 2, b * N:(b + 1) * N], I_[:])
                i.then_inc(rows_filled, 1)

            ring(pe, rows)

        @block.scalar
        def _(act):
            def dst_size(dst):
                n = 1
                for k in dst.shape[1:]:
                    n *= k
                return n

            def move(step, h, t, dst, name, func=ACT.Copy, j=0):
                wait_filled(act, step, h, t, j)
                src = bank_of(step, h, j)[:, 0:dst_size(dst)].rearrange("p (b n) -> p b n", b=dst.shape[1])
                act.activation(dst, src, func).then_inc(ready[name], 1)

            def fused_step(step, h, t):
                n = half_number(step, t, h) if step not in ("gates", "tanhc") else None
                if step == "ax":
                    move(step, h, t, yT[:, h], "yT")
                if step == "h1":
                    for j in range(2):
                        move(step, h, t, h1[:, h, 2 * j:2 * j + 2, :], f"h1_{j}", ACT.Relu, j)
                if step == "z":
                    move(step, h, t, z[:, h], "z")
                if step == "gax":
                    move(step, h, t, yT[:, h], "gyT")
                if step == "gh":
                    move(step, h, t, h1[:, h, :, 0:D], "gh1", ACT.Relu)
                if step == "ah1":
                    for k in range(2):
                        move(step, h, t, y2T[:, HI, k], f"y2T_hi{k}", ACT.Copy, k)
                if step == "gah":
                    move(step, h, t, z[:, h], "gy2T")
                if step == "gx":
                    move(step, h, t, xl[:, HI, BH * h:BH * h + BH, :], "xl_hi", ACT.Relu)
                if step == "x2T":
                    move(step, h, t, x2T[:, h], "x2T")
                if step == "s1":
                    act.wait_ge(s1_filled, t - LAG[step] + 1)
                    act.activation(s1[:], s1_bank, ACT.Copy).then_inc(ready["s1"], 1)
                if step == "expo":
                    act.wait_ge(ready["nmax"], n + 1)
                    for b in range(BH):
                        i = act.activation(E[:, h, b, :], E[:, h, b, :], ACT.Exp, bias=nmax[:, h, b:b + 1],
                                           accum_out=psum_[:, h, b:b + 1])
                    i.then_inc(ready["P"], 1)
                if step == "gates":
                    if isinstance(t, int) and t == LAG[step] and h == 0:
                        act.wait_ge(bias_ready, 2)
                    p, _, _, nb = SLOTS[h]
                    width = nb * (N // p)
                    unit = t - LAG[step]
                    for i, g in enumerate(slot_gates(h)):
                        act.wait_ge(gates_filled, unit * GATES_BEFORE[NSLOT] + GATES_BEFORE[h] + i + 1)
                        act.activation(gact[:, 0:width] if g == GATE_G else G[:, g, 0:width],
                                       G[:, g, 0:width], ACT.Tanh,
                                       bias=gbias[:, p - 1, g:g + 1], scale=1.0 if g == GATE_G else 0.5)\
                            .then_inc(gates_done, 1)
                if step == "tanhc":
                    p, _, _, nb = SLOTS[h]
                    width = nb * (N // p)
                    act.wait_ge(cell_ready, (t - LAG[step]) * NSLOT + h + 1)
                    act.activation(tanhc[:, 0:width], cell[:, 0:width], ACT.Tanh, scale=0.5)\
                        .then_inc(tanhc_ready, 1)

            def body(t):
                for step, h in ORDER:
                    if present(step, t):
                        fused_step(step, h, t)

            act.wait_ge(setup_dve, SETUP_STEPS)
            act.wait_ge(loaded, NLOAD)
            for raw, parts, factor in SPLITS:
                act.activation(parts[:, HI, :], raw, ACT.Copy, scale=factor).then_inc(split_hi, 1)
            bodies(act, body)

            act.wait_ge(bn_dve, 6)
            for h in range(2):
                act.wait_ge(x3_stored[h], 16 * UNITS)

            def relu_group(g, r):
                wait(act, out_filled, late(g, g - RING + 1))
                for k in range(2):
                    act.wait_ge(hpre_filled, g * 2 + k + 1)
                    act.activation(relu[:, r, k, :], G[:, 2 * (r % 2) + k, :], ACT.Relu, bias=bn[:, 6 + k:7 + k],
                                   scale=bn[:, 8 + k:9 + k]).then_inc(relu_ready, 1)

            ring(act, relu_group)

            def affine(g, r):
                wait(act, rows_filled, g - 1 if not isinstance(g, int) or g >= 2 else 0)
                act.activation(oaff[:, r % 2, :], AGG[:, g, :], ACT.Identity, bias=bn[:, 14:15],
                               scale=bn[:, 13:14]).then_inc(affine_ready, 1)

            def finish(g, r):
                act.wait_ge(f_rstd, g + 1)
                if not isinstance(g, int) or g >= RING:
                    act.wait_ge(stored[r], (g - r) * (16 // RING))
                for b in range(BH):
                    i = act.activation(fin[:, r, b, :], res[:, r, b, :], ACT.Identity, bias=fnb[:, r, b:b + 1],
                                       scale=frs[:, r, b:b + 1])
                i.then_inc(fin_ready, 1)

            def one(g, r):
                affine(g, r)
                if not isinstance(g, int) or g >= 3:
                    finish(g - 3, (r - 3) % RING)

            act.wait_ge(bn_dve, 13)
            ring(act, one)
            for g in range(GROUPS - 3, GROUPS):
                finish(g, g % RING)

        @block.vector
        def _(dve):
            setup = [0]

            def chain(i):
                setup[0] += 1
                i.then_inc(setup_dve, 1)
                dve.wait_ge(setup_dve, setup[0])

            dve.wait_ge(loaded_first, NFIRST)
            dve.wait_ge(setup_pool, 4)
            chain(V.tensor_scalar(maskadd[:], A_[:], 0.0, MASKED, ALU.is_equal, ALU.mult))
            V.tensor_tensor(A2T[:], AT[:], AT[:], ALU.mult)
            V.tensor_tensor(ANT[:], AT[:], I_[:], ALU.add)
            chain(V.tensor_tensor(A_[:], A_[:], I_[:], ALU.add))
            chain(V.tensor_tensor(scratch[:], A_[:], I_[:], ALU.mult))
            for k, m in enumerate((ANT, A_, scratch)):
                i = V.tensor_reduce(deg[:, k:k + 1], m[:], axis=AX.X, op=ALU.add)
            chain(i)
            chain(V.tensor_tensor(deg[:, 3:4], deg[:, 0:1], deg[:, 1:2], ALU.add))
            chain(V.tensor_tensor(deg[:, 3:4], deg[:, 3:4], deg[:, 2:3], ALU.subtract))
            dve.wait_ge(setup_pool, 5)
            V.tensor_scalar(AHT[:], ANT[:], dinv[:], None, ALU.mult)
            chain(V.tensor_scalar(scratch[:], I_[:], dinv[:], None, ALU.mult))
            dve.wait_ge(setup_pe, 4)
            chain(V.tensor_tensor(AHT[:], F[:, 3, 0:N], AHT[:], ALU.mult))
            V.tensor_copy(rs_hl[:, HI, :], F[0:1, 0, 0:N])
            V.tensor_copy(bg_hl[:, :, HI, :], bg[:])
            V.tensor_copy(wa1[:], F[:, 1, 0:1])
            V.tensor_copy(I_r[:], I_[:])
            chain(V.tensor_copy(wa2[:], F[:, 2, 0:128]))
            V.tensor_tensor(rs_hl[:, LO, :], F[0:1, 0, 0:N], rs_hl[:, HI, :].bitcast(fp32), ALU.subtract)
            chain(V.tensor_tensor(bg_hl[:, :, LO, :], bg[:], bg_hl[:, :, HI, :].bitcast(fp32),
                                  ALU.subtract))

            biases = [0]

            def bias_chain(i):
                biases[0] += 1
                i.then_inc(bias_ready, 1)
                dve.wait_ge(bias_ready, biases[0])

            def split_weights(parts_of):
                for n in parts_of:
                    raw, parts, factor = SPLITS[n]
                    dve.wait_ge(split_hi, n + 1)
                    V.scalar_tensor_tensor(parts[:, LO, :], raw, factor, parts[:, HI, :].bitcast(fp32), ALU.mult,
                                           ALU.subtract).then_inc(split_lo, 1)

            def lstm_biases():
                dve.wait_ge(loaded, NLOAD)
                bias_chain(V.tensor_tensor(gbias[:], gbias[:], bhh[:], ALU.add))
                for g in (GATE_I, GATE_F, GATE_O):
                    i = V.tensor_scalar(gbias[:, :, g], gbias[:, :, g], 0.5, None, ALU.mult)
                bias_chain(i)

            def take(step, h, t, dst, name, j=0, relu_=False):
                wait_filled(dve, step, h, t, j)
                src = per_batch(bank_of(step, h, j))
                if relu_:
                    i = V.tensor_scalar(dst, src, 0.0, None, ALU.max)
                else:
                    i = V.tensor_copy(dst, src)
                i.then_inc(ready[name], 1)

            def stats(n, h, r, count):
                dve.wait_ge(added[n], count)
                for b in range(BH):
                    i = V.bn_stats(lnst[:, n, h, b, :], r[:, b, :])
                i.then_inc(stated[n], 1)
                dve.wait_ge(stated[n], count)
                V.tensor_copy(carry[:], lnst[:, n, h, 0, 0:1])
                for b in range(BH):
                    i = V.bn_aggr(lnmv[:, n, h, b, :], lnst[:, n, h, b, :])
                i.then_inc(aggregated[n], 1)

            def normalise(n, h, r, name, count):
                dve.wait_ge(rstd[n], count)
                for b in range(BH):
                    i = V.tensor_scalar(r[:, b, :], r[:, b, :], lnmv[:, n, h, b, 0:1], lnr[:, n, h, b:b + 1],
                                        ALU.subtract, ALU.mult)
                i.then_inc(ready[name], 1)

            def fused_step(step, h, t):
                lstm = step in ("gates", "tanhc", "hout")
                n = None if lstm else half_number(step, t, h)
                if step == "ah1":
                    for k in range(2):
                        dve.wait_ge(ready[f"y2T_hi{k}"], n + 1)
                        V.tensor_tensor(y2T[:, LO, k], per_batch(bank_of(step, h, k)),
                                        y2T[:, HI, k].bitcast(fp32), ALU.subtract).then_inc(ready[f"y2T_{k}"], 1)
                if step == "gx":
                    part = xl[:, :, BH * h:BH * h + BH, :]
                    dve.wait_ge(ready["xl_hi"], n + 1)
                    V.scalar_tensor_tensor(part[:, LO].rearrange("p b n -> p (b n)"), bank_of(step, h), 0.0,
                                           part[:, HI].bitcast(fp32).rearrange("p b n -> p (b n)"),
                                           ALU.max, ALU.subtract).then_inc(ready["xl"], 1)
                if step in ("h2a", "h2b"):
                    for j in range(2):
                        c = j + 2 * (step == "h2b")
                        take(step, h, t, h2T[:, c], f"h2T_{c}", j, True)
                if step == "oz":
                    if not isinstance(t, int) or t > 0:
                        dve.wait_ge(ready["x1_kept"], n - 1)
                    wait_filled(dve, step, h, t)
                    V.tensor_tensor(x1[:, h], per_batch(bank_of(step, h)), xin[:, h], ALU.add)\
                        .then_inc(added[0], 1)
                for k, r in enumerate((x1, x2, x2)):
                    if step == f"stats{k + 1}":
                        stats(k, h, r[:, h], n + 1)
                if step == "norm1":
                    normalise(0, h, x1[:, h], "x1", n + 1)
                if step == "backT":
                    wait_filled(dve, step, h, t)
                    dve.wait_ge(ready["x1_kept"], n + 1)
                    if not isinstance(t, int) or t > LAG[step]:
                        dve.wait_ge(x3_stored[h], (t - LAG[step]) * 16)
                    V.scalar_tensor_tensor(x2[:, h].rearrange("p b d -> p (b d)"), bank_of(step, h), 0.5,
                                           AGG[:, n, :], ALU.mult, ALU.add).then_inc(added[1], 1)
                if step == "norm2":
                    normalise(1, h, x2[:, h], "x2", n + 1)
                if step == "wh":
                    take(step, h, t, wh[:, h], "wh")
                if step == "s2":
                    wait_filled(dve, step, h, t)
                    dve.wait_ge(ready["s1"], t - LAG[step] + 1)
                    o = per_batch(bank_of(step, h))
                    for b in range(BH):
                        i = V.scalar_tensor_tensor(E[:, h, b, :], o[:, b, :], s1[:, BH * h + b:BH * h + b + 1], maskadd[:],
                                                   ALU.add, ALU.add)
                    i.then_inc(ready["E"], 1)
                if step == "lrelu":
                    dve.wait_ge(ready["E"], n + 1)
                    V.scalar_tensor_tensor(E[:, h], E[:, h], ALPHA, E[:, h], ALU.mult, ALU.max)\
                        .then_inc(ready["L"], 1)
                if step == "rowmax":
                    dve.wait_ge(ready["L"], n + 1)
                    V.tensor_reduce(nmax[:, h], E[:, h], axis=AX.X, op=ALU.max, negate=True)\
                        .then_inc(ready["nmax"], 1)
                if step == "pT":
                    take(step, h, t, x2T[:, h], "PT")
                    dve.wait_ge(ready["P"], n + 1)
                    V.reciprocal(rsum[:, h], psum_[:, h]).then_inc(ready["rsum"], 1)
                if step == "att":
                    wait_filled(dve, step, h, t)
                    dve.wait_ge(ready["rsum"], n + 1)
                    o = per_batch(bank_of(step, h))
                    for b in range(BH):
                        i = V.scalar_tensor_tensor(x2[:, h, b, :], o[:, b, :], rsum[:, h, b:b + 1],
                                                   x2[:, h, b, :], ALU.mult, ALU.add)
                    i.then_inc(added[2], 1)
                if step == "norm3":
                    normalise(2, h, x2[:, h], "x3", n + 1)
                if step == "agg":
                    wait_filled(dve, step, h, t)
                    V.tensor_scalar(AGG[:, n, :], bank_of(step, h), 1.0, None, ALU.mult).then_inc(ready["agg"], 1)
                if step == "stat":
                    for k in range(2):
                        dve.wait_ge(setup_dve, SETUP_STEPS)
                        wait_filled(dve, step, h, t, k)
                        V.bn_stats(stats1[:, k, n, :], bank_of(step, h, k)).then_inc(ready["stat"], 1)
                if step == "gates":
                    p, later, _, nb = SLOTS[h]
                    w = nb * (N // p)
                    unit = t - LAG[step]
                    done = unit * GATES_BEFORE[NSLOT] + GATES_BEFORE[h]
                    dve.wait_ge(gates_done, done + 2)
                    if not later:
                        V.scalar_tensor_tensor(cell[:, 0:w], G[:, GATE_I, 0:w], 1.0, gact[:, 0:w],
                                               ALU.add, ALU.mult).then_inc(cell_ready, 1)
                    else:
                        V.scalar_tensor_tensor(gact[:, 0:w], G[:, GATE_I, 0:w], 1.0, gact[:, 0:w],
                                               ALU.add, ALU.mult).then_inc(terms_done, 1)
                        dve.wait_ge(gates_done, done + 3)
                        V.scalar_tensor_tensor(cell[:, 0:w], G[:, GATE_F, 0:w], 1.0, cell[:, 0:w],
                                               ALU.add, ALU.mult).then_inc(terms_done, 1)
                        dve.wait_ge(terms_done, unit * 2 * LATER_BEFORE[NSLOT] + 2 * LATER_BEFORE[h] + 2)
                        V.scalar_tensor_tensor(cell[:, 0:w], cell[:, 0:w], 0.5, gact[:, 0:w],
                                               ALU.mult, ALU.add).then_inc(cell_ready, 1)
                if step == "hout":
                    p, _, _, nb = SLOTS[h]
                    w = nb * (N // p)
                    unit = t - LAG[step]
                    dve.wait_ge(tanhc_ready, unit * NSLOT + h + 1)
                    V.scalar_tensor_tensor(hnew[:, 0:w], G[:, GATE_O, 0:w], 1.0, tanhc[:, 0:w],
                                           ALU.add, ALU.mult).then_inc(h_made, 1)
                    src, dst = h_views(h)
                    dve.wait_ge(h_made, unit * NSLOT + h + 1)
                    V.tensor_copy(dst[HI], src).then_inc(h_hi, 1)
                    dve.wait_ge(h_hi, unit * NSLOT + h + 1)
                    V.tensor_tensor(dst[LO], src, dst[HI].bitcast(fp32), ALU.subtract).then_inc(h_ready, 1)

            def body(t):
                for step, h in ORDER:
                    if present(step, t):
                        fused_step(step, h, t)
                    if isinstance(t, int) and t == 0 and (step, h) == ("ax", 1):
                        split_weights(range(2))
                    if isinstance(t, int) and t == 0 and (step, h) == ("h2b", 0):
                        split_weights(range(2, len(SPLITS)))
                        lstm_biases()

            bodies(dve, body)

            bns = [0]

            def bn_chain(i):
                bns[0] += 1
                i.then_inc(bn_dve, 1)
                dve.wait_ge(bn_dve, bns[0])

            dve.wait_ge(ready["stat"], 4 * UNITS)
            mv = scratch[:, 0:4].rearrange("p (k c) -> p k c", k=2)
            for k in range(2):
                i = V.bn_aggr(mv[:, k, :], stats1[:, k].rearrange("p g s -> p (g s)"))
            bn_chain(i)
            bn_chain(V.tensor_tensor(bn[:, 0:2], mv[:, :, 0], vec1[:, 0, :], ALU.add))
            bn_chain(V.tensor_scalar(bn[:, 2:4], mv[:, :, 1], EPS, None, ALU.add))
            dve.wait_ge(bn_pool, 1)
            bn_chain(V.tensor_tensor(bn[:, 8:10], bn[:, 4:6], vec1[:, 1, :], ALU.mult))
            bn_chain(V.tensor_tensor(bn[:, 0:2], vec1[:, 0, :], bn[:, 0:2], ALU.subtract))
            V.tensor_tensor(bn[:, 0:2], bn[:, 0:2], bn[:, 8:10], ALU.mult).then_inc(shift_term, 1)
            dve.wait_ge(shift_term, 1)
            bn_chain(V.tensor_tensor(bn[:, 6:8], bn[:, 0:2], vec1[:, 2, :], ALU.add))

            def keep(g, r):
                dve.wait_ge(out_filled, g + 1)
                V.tensor_scalar(AGG[:, g, :], F[:, r, :], 1.0, None, ALU.mult)
                V.bn_stats(stats2[:, g, :], F[:, r, :]).then_inc(out_kept, 1)

            ring(dve, keep)

            dve.wait_ge(out_kept, GROUPS)
            bn_chain(V.bn_aggr(scratch[:, 8:10], stats2[:].rearrange("p g s -> p (g s)")))
            bn_chain(V.tensor_tensor(bn[:, 10:11], scratch[:, 8:9], vec2[:, 0, :], ALU.add))
            bn_chain(V.tensor_tensor(bn[:, 10:11], vec2[:, 0, :], bn[:, 10:11], ALU.subtract))
            bn_chain(V.tensor_scalar(bn[:, 11:12], scratch[:, 9:10], EPS, None, ALU.add))
            dve.wait_ge(bn_pool, 2)
            bn_chain(V.tensor_tensor(bn[:, 13:14], bn[:, 12:13], vec2[:, 1, :], ALU.mult))
            bn_chain(V.tensor_tensor(bn[:, 10:11], bn[:, 10:11], bn[:, 13:14], ALU.mult))
            bn_chain(V.tensor_tensor(bn[:, 14:15], bn[:, 10:11], vec2[:, 2, :], ALU.add))

            def residual(g, r):
                wait(dve, fin_ready, late(g, g - RING + 1))
                dve.wait_ge(rows_filled, g + 1)
                V.tensor_tensor(res[:, r].rearrange("p b d -> p (b d)"), F[:, r, :],
                                X3[:, g, :], ALU.add).then_inc(res_ready, 1)
                dve.wait_ge(res_ready, g + 1)
                for b in range(BH):
                    i = V.bn_stats(fst[:, r, b, :], res[:, r, b, :])
                i.then_inc(f_stats, 1)
                dve.wait_ge(f_stats, g + 1)
                V.tensor_copy(carry[:], fst[:, r, 0, 0:1])
                for b in range(BH):
                    i = V.bn_aggr(fmv[:, r, b, :], fst[:, r, b, :])
                i.then_inc(f_mv, 1)

            for h in range(2):
                dve.wait_ge(x3_stored[h], 16 * UNITS)
            dve.wait_ge(x3_back, 16 * 8)
            ring(dve, residual)


def kernel(**inputs):
    import numpy as np
    import concourse.bacc as bacc
    from concourse import mybir as mb
    from concourse.bass_utils import run_bass_kernel_spmd as run

    i = {k: np.asarray(v) for k, v in inputs.items()}
    cols = lambda a, k: a.reshape(k, 128).T
    data = {
        "x": i["x"].reshape(GROUPS, BH, N, D).transpose(0, 2, 1, 3).reshape(GROUPS, N, BH, D),
        "adj": i["adj"], "adjT": i["adj"].T,
        "l0_w1": i["L0_gnn_W1"],
        "l0_w2": i["L0_gnn_W2"].reshape(2, 128, HID2).transpose(1, 0, 2),
        "l0_w3": i["L0_gnn_W3"].reshape(4, 128, D).transpose(1, 0, 2),
        "l1_wg0": i["L1_gnn_Wg0"], "l1_bg0": i["L1_gnn_bg0"].reshape(1, D),
        "l1_wg1": i["L1_gnn_Wg1"], "l1_bg1": i["L1_gnn_bg1"].reshape(1, D),
        "l1_wihT": i["L1_gnn_Wih"].transpose(2, 0, 1), "l1_whhT": i["L1_gnn_Whh"].transpose(2, 0, 1),
        "l1_bih": i["L1_gnn_bih"].reshape(SKIPS, 4, D).transpose(2, 0, 1),
        "l1_bhh": i["L1_gnn_bhh"].reshape(SKIPS, 4, D).transpose(2, 0, 1),
        "l2_w": i["L2_gnn_W"], "l2_wT": i["L2_gnn_W"].T, "l2_a": cols(i["L2_gnn_a"], 2),
        "l3_w1T": i["L3_gnn_W1"].T,
        "l3_vec1": np.stack([cols(i[f"L3_gnn_{n}"], 2) for n in ("b1", "g1", "be1")], 1),
        "l3_w2T": i["L3_gnn_W2"].T.reshape(2, 128, D).transpose(1, 0, 2),
        "l3_vec2": np.stack([cols(i[f"L3_gnn_{n}"], 1) for n in ("b2", "g2", "be2")], 1),
        "eye": np.eye(128, dtype=np.float32),
    }
    nc = bacc.Bacc("TRN2", target_bir_lowering=False, num_devices=1)
    arrays, args = {}, []
    for name, a in data.items():
        a = np.ascontiguousarray(a)
        arrays[f"in_{name}"] = a
        args.append(nc.dram_tensor(f"in_{name}", a.shape, mb.dt.from_np(a.dtype), kind="ExternalInput").ap())
    out = nc.dram_tensor("out_rows", (GROUPS, N, BH, D), mb.dt.float32, kind="ExternalOutput").ap()
    build_adj_resnorm_d4(nc, *args, out)
    r = run(nc, [arrays], core_ids=[0])
    o = r.results[0]["out_rows"]
    return o.transpose(0, 2, 1, 3).reshape(B, N, D)
```

```python
import concourse.bass as bass
from concourse import mybir
from contextlib import ExitStack

B, N, D = 128, 128, 128
BH = 4
COLS = BH * N
UB = 2 * BH
UNITS = B // UB
GROUPS = B // BH
HID1, HID2 = 256, 512
SKIPS = 4
RING = 4
VECTOR_PLACE = 3
EARLY_PARTS = 6
TAIL = 8
BEHIND = 4
PEEL = 8
EPS = 1e-5
ALPHA = 0.2
MASKED = -1.0e30
GATE_I, GATE_F, GATE_G, GATE_O = range(4)

SLOTS = [(1, 0, 0, BH), (1, 0, BH, BH)] + [(p, s, 0, UB) for p in range(2, SKIPS + 1) for s in range(p)]
NSLOT = len(SLOTS)


def slot_gates(s):
    return [GATE_I, GATE_G, GATE_O] if SLOTS[s][1] == 0 else [GATE_I, GATE_G, GATE_F, GATE_O]


GATES_BEFORE = [sum(len(slot_gates(k)) for k in range(s)) for s in range(NSLOT + 1)]
LATER_BEFORE = [sum(SLOTS[k][1] > 0 for k in range(s)) for s in range(NSLOT + 1)]

ORDER = [
    ("stats2", 0),
    ("gates", 0), ("ax", 0), ("tanhc", 0), ("stats2", 1), ("norm2", 0), ("ax", 1), ("h1", 0), ("hout", 0),
    ("gates", 1), ("norm2", 1), ("tanhc", 1), ("hout", 1), ("x2T", 0), ("h1", 1), ("s1", 0), ("x2T", 1),
    ("s1", 1), ("wh", 0),
    ("gates", 2), ("tanhc", 2), ("hout", 2), ("wh", 1), ("s2", 0), ("s2", 1), ("ah1", 0), ("lrelu", 0),
    ("inputs", 3), ("rowmax", 0), ("lrelu", 1),
    ("gates", 3), ("tanhc", 3), ("hout", 3), ("expo", 0), ("h2a", 0), ("rowmax", 1), ("h2b", 0),
    ("gates", 4), ("ah1", 1), ("tanhc", 4), ("hout", 4), ("expo", 1), ("inputs", 5), ("z", 0),
    ("gates", 5), ("tanhc", 5), ("hout", 5), ("pT", 0), ("pT", 1), ("h2a", 1), ("inputs", 6),
    ("gates", 6), ("att", 0), ("tanhc", 6), ("hout", 6), ("stats3", 0), ("att", 1), ("h2b", 1),
    ("gates", 7), ("stats3", 1), ("oz", 0), ("tanhc", 7), ("hout", 7), ("z", 1), ("stats1", 0), ("norm3", 0),
    ("norm3", 1), ("inputs", 8), ("norm1", 0),
    ("gates", 8), ("tanhc", 8), ("oz", 1), ("hout", 8), ("stats1", 1), ("agg", 0), ("gax", 0), ("agg", 1),
    ("inputs", 9),
    ("gates", 9), ("tanhc", 9), ("norm1", 1), ("gh", 0), ("hout", 9), ("stat", 0), ("inputs", 10),
    ("gates", 10), ("tanhc", 10), ("hout", 10), ("gax", 1), ("stat", 1), ("gah", 0), ("gh", 1), ("backT", 0),
    ("gah", 1), ("gx", 0), ("backT", 1), ("gx", 1),
]
FILLS = {"ax": 1, "h1": 2, "ah1": 2, "h2a": 2, "h2b": 2, "z": 1, "oz": 1, "gax": 1, "gh": 1, "gah": 1, "gx": 1,
         "backT": 1, "x2T": 1, "wh": 1, "s2": 1, "pT": 1, "att": 1, "agg": 1, "stat": 2}
LAG = {s: 0 for s in ("ax", "stats1", "h1", "ah1", "h2a", "h2b", "z", "oz", "norm1", "gax", "gh", "gah", "gx")}
LAG |= {s: 1 for s in ("inputs", "gates", "tanhc", "hout", "backT")}
LAG |= {s: 2 for s in ("s1", "stats2", "stats3", "norm2", "x2T", "wh", "s2", "lrelu", "rowmax", "expo", "pT", "att",
                        "norm3", "agg", "stat")}
NBANK = 4
SCALAR_MOVES = {("ax", 0), ("h1", 0), ("h1", 1), ("z", 0), ("gax", 0), ("gh", 0), ("x2T", 0),
                ("h2a", 1), ("h2b", 0), ("h2b", 1), ("wh", 0), ("pT", 0)}
VECTOR_MOVES = {("h2a", 0)}
SETUP_STEPS = 11
BODIES = UNITS + 2
LOOP0, LOOP1 = 3, UNITS


def active(step, t):
    return 0 <= t - LAG[step] < UNITS


FILL_LIST = [(s, h, j) for s, h in ORDER if s in FILLS for j in range(FILLS[s])]
BANK = {f: i % NBANK for i, f in enumerate(FILL_LIST)}
PER_BODY = [sum(BANK[f] == k for f in FILL_LIST) for k in range(NBANK)]


def fills_in(t, bank, upto=None):
    n = 0
    for f in FILL_LIST:
        if f == upto:
            break
        n += BANK[f] == bank and active(f[0], t)
    return n


def fill_number(f, t):
    bank = BANK[f]
    if isinstance(t, int):
        return sum(fills_in(q, bank) for q in range(t)) + fills_in(t, bank, f) + 1
    base = sum(fills_in(q, bank) for q in range(LOOP0)) + fills_in(LOOP0, bank, f) + 1
    return (t - LOOP0) * PER_BODY[bank] + base


def fill_before(f, t):
    q, at = (t, t) if isinstance(t, int) else (LOOP0, t)
    while q >= 0:
        here = [e for e in FILL_LIST if BANK[e] == BANK[f] and active(e[0], q)]
        if f in here and at is t:
            here = here[:here.index(f)]
        if here:
            return here[-1], at
        q, at = q - 1, at - 1
    return None


def build_adj_resnorm_d4(nc, x, adj, adjT, l0_w1, l0_w2, l0_w3, l1_wg0, l1_bg0, l1_wg1, l1_bg1, l1_wihT, l1_whhT,
                         l1_bih, l1_bhh, l2_w, l2_wT, l2_a, l3_w1T, l3_vec1, l3_w2T, l3_vec2, eye, out):
    fp32 = mybir.dt.float32
    fp32r = mybir.dt.float32r
    HI, LO = 0, 1
    PASSES = ((HI, HI), (LO, HI), (HI, LO))
    ALU = mybir.AluOpType
    ACT = mybir.ActivationFunctionType
    AX = mybir.AxisListType
    V = nc.vector

    ctx = ExitStack()
    with ctx:
        def sb(name, shape, dt=fp32, where=ctx):
            return where.enter_context(nc.sbuf_tensor(name, shape, dt))

        def twins(name, shape, where=ctx):
            with ExitStack() as first:
                plain = sb(name, shape, fp32, first)
            return plain, sb(name + "_parts", shape, fp32r, where)

        def sem(name):
            return ctx.enter_context(nc.semaphore(name))

        AT = sb("AT", [128, N])
        A2T = sb("A2T", [128, N])
        AHT = sb("AHT", [128, N])
        I_ = sb("I_", [128, 128])
        I_r = sb("I_r", [128, 128], fp32r)
        maskadd = sb("maskadd", [128, N])
        w1 = sb("w1", [128, HID1])
        w2 = sb("w2", [128, 2, 2, HID2], fp32r)
        w3 = sb("w3", [128, 4, D])
        wg0 = sb("wg0", [128, D])
        wg1 = sb("wg1", [128, 2, D], fp32r)
        bg = sb("bg", [1, 2, D])
        bg_hl = sb("bg_hl", [1, 2, 2, D], fp32r)
        rs_hl = sb("rs_hl", [1, 2, N], fp32r)
        rs4 = sb("rs4", [4, 1, N], fp32r)
        bg4 = sb("bg4", [4, 2, D], fp32r)
        wih = sb("wih", [128, 2, SKIPS, 4 * D], fp32r)
        whh = sb("whh", [128, 2, SKIPS - 1, 4 * D], fp32r)
        gbias = sb("gbias", [128, SKIPS, 4])
        bhh = sb("bhh", [128, SKIPS, 4])
        w_l2 = sb("w_l2", [128, D])
        a12 = sb("a12", [128, 2])
        wa1 = sb("wa1", [128, D])
        wa2 = sb("wa2", [128, 128])
        w1T_l3 = sb("w1T_l3", [128, 2, HID1], fp32r)
        w2T_l3 = sb("w2T_l3", [128, 2, D])
        vec1 = sb("vec1", [128, 3, 2])
        vec2 = sb("vec2", [128, 3, 1])
        ones = sb("ones", [128, 128])
        scratch = sb("scratch", [128, 128])
        deg = sb("deg", [128, 4])
        dinv = sb("dinv", [128, 1])
        eps4 = sb("eps4", [128, BH])
        mhalf = sb("mhalf", [128, BH])
        AGG, AGG_r = twins("AGG", [128, GROUPS, COLS])
        stats1 = sb("stats1", [128, 2, GROUPS, 6])
        stats2 = sb("stats2", [128, GROUPS, 6])
        bn = sb("bn", [128, 16])
        fst = sb("fst", [128, TAIL, BH, 6])
        fmv = sb("fmv", [128, TAIL, BH, 2])
        fve = sb("fve", [128, TAIL, BH])
        frs = sb("frs", [128, TAIL, BH])
        fnm = sb("fnm", [128, TAIL, BH])
        fnb = sb("fnb", [128, TAIL, BH])
        mone = sb("mone", [128, BH])
        lnst = sb("lnst", [128, 3, 2, BH, 6])
        lnmv = sb("lnmv", [128, 3, 2, BH, 2])
        lnve = sb("lnve", [128, 3, 2, BH])
        lnr = sb("lnr", [128, 3, 2, BH])
        carry = sb("carry", [128, 1])
        s1 = sb("s1", [128, UB])
        nmax = sb("nmax", [128, 2, BH])
        psum_ = sb("psum_", [128, 2, BH])
        rsum = sb("rsum", [128, 2, BH])

        fused = ExitStack()
        with fused:
            def fb(name, shape):
                return sb(name, shape, fp32, fused)

            def fr(name, shape):
                return sb(name, shape, fp32r, fused)

            xin = fb("xin", [128, 2, BH, D])
            yT = fb("yT", [128, 2, BH, N])
            h1, h1_r = twins("h1", [128, 2, BH, HID1], fused)
            y2T = fr("y2T", [128, 2, 2, BH, N])
            h2T = fb("h2T", [128, 4, BH, N])
            z, z_r = twins("z", [128, 2, BH, D], fused)
            x1 = fb("x1", [128, 2, BH, D])
            xl = fr("xl", [128, 2, UB, N])
            x2 = fb("x2", [128, 2, BH, D])
            x2T, x2T_r = twins("x2T", [128, 2, BH, N], fused)
            wh = fb("wh", [128, 2, BH, D])
            E = fb("E", [128, 2, BH, N])
            gact = fb("gact", [128, COLS])
            cell = fb("cell", [128, COLS])
            tanhc = fb("tanhc", [128, COLS])
            hnew = fb("hnew", [128, COLS])
            hs = fr("hs", [128, 2, COLS])
            HT = fr("HT", [128, 2, UB, N])
        X3 = sb("X3", [128, GROUPS, COLS])
        features_only = ExitStack()
        with features_only:
            relu = sb("relu", [128, RING, 2, COLS], fp32, features_only)
        oaff = sb("oaff", [128, RING, COLS])
        fin = sb("fin", [128, RING, BH, D])

        G = ctx.enter_context(nc.psum_tensor("G", [128, 4, COLS], fp32))
        F = ctx.enter_context(nc.psum_tensor("F", [128, NBANK, COLS], fp32))
        x3_dram = nc.dram_tensor("x3_dram", (GROUPS, 128, COLS), fp32, kind="Internal").ap()
        hpre_dram = nc.dram_tensor("hpre_dram", (GROUPS, 128, COLS), fp32, kind="Internal").ap()

        adjT_loaded = sem("adjT_loaded")
        loaded_first = sem("first_loaded")
        loaded_second = sem("second_loaded")
        loaded = sem("weights_loaded")
        rows_built = sem("bias_rows_built")
        split_hi, split_lo = sem("weights_hi_ready"), sem("weights_lo_ready")
        filled = [sem(f"bank{k}_filled") for k in range(NBANK)]
        x_loaded = [sem(f"x_half{h}_loaded") for h in range(2)]
        names = ["yT", "h1_0", "h1_1", "y2T_0", "y2T_1", "h2T_0", "h2T_1", "h2T_2", "h2T_3", "z", "x1",
                 "x1_kept", "gyT", "gh1", "gy2T", "xl", "x2", "x2T", "wh", "s1", "E", "L", "nmax", "P",
                 "rsum", "PT", "x3", "agg", "stat", "hpre", "y2T_hi0", "y2T_hi1", "xl_hi", "gy2T_hi", "agg_hi"]
        ready = {n: sem(f"{n}_ready") for n in names}
        added = [sem(f"ln{n}_added") for n in range(3)]
        stated = [sem(f"ln{n}_stats") for n in range(3)]
        aggregated = [sem(f"ln{n}_mean_var") for n in range(3)]
        eps_added = [sem(f"ln{n}_eps_added") for n in range(3)]
        rstd = [sem(f"ln{n}_rstd") for n in range(3)]
        gates_filled = sem("gates_filled")
        gates_done = sem("gates_done")
        terms_done = sem("cell_terms_done")
        cell_ready = sem("cell_ready")
        tanhc_ready = sem("tanhc_ready")
        h_made = sem("lstm_h_made")
        h_hi = sem("lstm_h_hi_ready")
        h_ready = sem("lstm_h_lo_ready")
        hpre_stored = [sem(f"hpre_half{h}_stored") for h in range(2)]
        x3_stored = [sem(f"x3_half{h}_stored") for h in range(2)]
        setup_dve = sem("setup_dve")
        setup_pe = sem("setup_pe")
        setup_pool = sem("setup_pool")
        bn_dve = sem("bn_dve")
        shift_term = sem("shift_term")
        bias_ready = sem("lstm_bias_ready")
        bn_pool = sem("bn_pool")
        hpre_early, hpre_late = sem("hpre_early_parts_back"), sem("hpre_late_parts_back")
        affine_ready = sem("affine_ready")
        relu_ready = sem("relu_ready")
        out_filled = sem("out_filled")
        out_kept = sem("out_kept")
        x3_back = sem("x3_back")
        rows_filled = sem("rows_filled")
        f_stats, f_mv, f_eps, f_rstd = sem("fin_stats"), sem("fin_mean_var"), sem("fin_eps_added"), sem("fin_rstd")
        f_pow = sem("fin_pow")
        fin_ready = [sem(f"fin_ring{r}_ready") for r in range(RING)]
        stored = [sem(f"out_ring{r}_stored") for r in range(RING)]

        w2_raw = AGG[:, 0:2, :]
        wih_raw = AGG[:, 2:2 + SKIPS, :]
        whh_raw = AGG[:, 2 + SKIPS:1 + 2 * SKIPS, :]
        wg1_raw = AGG[:, 1 + 2 * SKIPS, 0:D]
        w1T_raw = AGG[:, 2 + 2 * SKIPS, 0:HID1]
        A_ = AGG[:, 3 + 2 * SKIPS, 0:N]
        ANT = AGG[:, 3 + 2 * SKIPS, N:2 * N]
        w_l2T = AGG[:, 3 + 2 * SKIPS, 2 * N:2 * N + D]
        FIRST_LOADS = [(w1, l0_w1), (A_, adj), (I_, eye), (w_l2T, l2_wT), (a12, l2_a),
                       (bg[:, 0, :], l1_bg0), (bg[:, 1, :], l1_bg1)]
        SECOND_LOADS = [(w2_raw, l0_w2), (wg1_raw, l1_wg1)]
        LOADS = [(w3, l0_w3), (wih_raw, l1_wihT), (whh_raw, l1_whhT[:, 1:SKIPS, :]),
                 (wg0, l1_wg0), (gbias, l1_bih), (bhh, l1_bhh), (w_l2, l2_w),
                 (w1T_raw, l3_w1T), (w2T_l3, l3_w2T), (vec1, l3_vec1), (vec2, l3_vec2)]
        SPLITS = [(w2_raw[:, k, :], w2[:, :, k, :], 1.0) for k in range(2)]
        SPLITS += [(wg1_raw, wg1, 1.0)]
        SPLITS += [(wih_raw[:, p, :], wih[:, :, p, :], 0.5 if p else 1.0) for p in range(SKIPS)]
        SPLITS += [(whh_raw[:, p, :], whh[:, :, p, :], 0.5) for p in range(SKIPS - 1)]
        SPLITS += [(w1T_raw, w1T_l3, 1.0)]
        NFIRST, NLOAD = 16 * len(FIRST_LOADS), 16 * len(LOADS)

        def wait(eng, s, n):
            if not isinstance(n, int) or n > 0:
                eng.wait_ge(s, n)

        def bodies(eng, body):
            for t in range(LOOP0):
                body(t)
            with eng.Fori(LOOP0, LOOP1) as t:
                body(t)
            for t in range(LOOP1, BODIES):
                body(t)

        def ring(eng, one, size=RING):
            for g in range(PEEL):
                one(g, g % size)
            with eng.Fori(PEEL, GROUPS - size + 1, size) as g:
                for r in range(size):
                    one(g + r, r)

        def tail_bank(r):
            return F[:, r, :] if r < NBANK else G[:, r - NBANK, :]

        def wait_fin(eng, g, r, back=0):
            if not isinstance(g, int) or g >= back:
                eng.wait_ge(fin_ready[r % RING], g - back - r % RING + 4)

        def late(g, n):
            return n if not isinstance(g, int) or g >= RING else 0

        def present(step, t):
            return not isinstance(t, int) or active(step, t)

        def half_number(step, t, h):
            return (t - LAG[step]) * 2 + h

        def bank_of(step, h, j=0):
            return F[:, BANK[(step, h, j)], :]

        def wait_filled(eng, step, h, t, j=0):
            f = (step, h, j)
            eng.wait_ge(filled[BANK[f]], fill_number(f, t))

        PRODUCT = {"ax": "yT", "z": "z", "gax": "gyT", "gh": "gh1", "gah": "gy2T", "gx": "xl", "x2T": "x2T",
                   "wh": "wh",
                   "s2": "E", "pT": "PT", "agg": "agg"}
        PRODUCTS = {"h1": ("h1_0", "h1_1"), "ah1": ("y2T_0", "y2T_1"), "h2a": ("h2T_0", "h2T_1"),
                    "h2b": ("h2T_2", "h2T_3")}
        SUMS = {"oz": 0, "backT": 1, "att": 2}

        def read_signal(f, t):
            step, h, j = f
            n = half_number(step, t, h)
            if step == "stat":
                return ready["hpre"], 2 * n + j + 1
            if step == "z":
                return ready["z"], n + 1
            if step in SUMS:
                return added[SUMS[step]], n + 1
            return ready[PRODUCT[step] if step in PRODUCT else PRODUCTS[step][j]], n + 1

        def h_views(s):
            p, step, b0, nb = SLOTS[s]
            nw = N // p
            src = hnew[:, 0:nb * nw].rearrange("p (b w) -> p b w", b=nb)
            if step == p - 1:
                return src, [HT[:, d, b0:b0 + nb, p - 1:nw * p:p] for d in (HI, LO)]
            return src, [hs[:, d, 0:nb * nw].rearrange("p (b w) -> p b w", b=nb) for d in (HI, LO)]

        def per_batch(ap):
            return ap.rearrange("p (b n) -> p b n", b=BH)

        def moved(step, h, n, j):
            if step in ("ax", "gax"):
                return yT[:, h], "yT" if step == "ax" else "gyT", False
            if step == "h1":
                return h1[:, h, 2 * j:2 * j + 2, :], f"h1_{j}", True
            if step in ("h2a", "h2b"):
                c = j + 2 * (step == "h2b")
                return h2T[:, c], f"h2T_{c}", True
            if step == "z":
                return z[:, h], "z", False
            if step == "gh":
                return h1[:, h, :, 0:D], "gh1", True
            if step in ("x2T", "pT"):
                return x2T[:, h], "x2T" if step == "x2T" else "PT", False
            return wh[:, h], "wh", False

        def gah_parts(h):
            return z_r[:, h], h1_r[:, h, :, D:2 * D]

        def agg_parts(h, n):
            return per_batch(AGG_r[:, n, :]), x2T_r[:, h]

        def moves(step, mine):
            return [j for j in range(FILLS.get(step, 0)) if (step, j) in mine]

        block = ctx.enter_context(nc.Block())

        @block.sync
        def _(sp):
            sp.dma_start(AT[:], adjT).then_inc(adjT_loaded, 16)
            for h in range(2):
                sp.dma_start(xin[:, h], x[h]).then_inc(x_loaded[h], 16)
            for dst, src in FIRST_LOADS:
                sp.dma_start(dst[:] if dst.__class__ is not bass.AP else dst, src).then_inc(loaded_first, 16)
            for dst, src in SECOND_LOADS:
                sp.dma_start(dst, src).then_inc(loaded_second, 16)
            for dst, src in LOADS:
                sp.dma_start(dst[:] if dst.__class__ is not bass.AP else dst, src).then_inc(loaded, 16)
            sp.wait_ge(setup_dve, SETUP_STEPS)
            for k in range(4):
                sp.dma_start(rs4[k:k + 1, 0, :].bitcast(fp32), rs_hl[:, k // 2, :].bitcast(fp32))\
                  .then_inc(rows_built, 16)
                sp.dma_start(bg4[k:k + 1, :, :].bitcast(fp32), bg_hl[:, :, k % 2, :].bitcast(fp32))\
                  .then_inc(rows_built, 16)

            def body(t):
                for step, h in ORDER:
                    if not present(step, t):
                        continue
                    if step == "oz" and (not isinstance(t, int) or t + 1 < UNITS):
                        sp.wait_ge(added[0], half_number(step, t, h) + 1)
                        sp.dma_start(xin[:, h], x[(t + 1) * 2 + h]).then_inc(x_loaded[h], 16)
                    if step == "norm3":
                        sp.wait_ge(ready["x3"], half_number(step, t, h) + 1)
                        sp.dma_start(x3_dram[half_number(step, t, h)],
                                     x2[:, h]).then_inc(x3_stored[h], 16)
                    if step == "stat":
                        n = half_number(step, t, h)
                        sp.wait_ge(ready["stat"], 2 * n + 1)
                        sp.dma_start(hpre_dram[n], E[:, h]).then_inc(hpre_stored[h], 16)

            for t in range(LOOP0):
                body(t)
            with sp.Fori(LOOP0, LOOP1 - 1) as t:
                body(t)
            for t in range(LOOP1 - 1, BODIES - 1):
                body(t)

            parts = 8
            q = GROUPS // parts

            def load_back(src, i, signal):
                sp.dma_start(X3[:, i * q:(i + 1) * q, :],
                             src[i * q:(i + 1) * q].rearrange("g p c -> p g c")).then_inc(signal, 16)

            sp.wait_ge(h_ready, UNITS * NSLOT)
            sp.wait_ge(ready["x1_kept"], 2 * UNITS)
            for h in range(2):
                sp.wait_ge(hpre_stored[h], 16 * EARLY_PARTS * q // 2)
            for i in range(EARLY_PARTS):
                load_back(hpre_dram, i, hpre_early)
            body(BODIES - 1)
            sp.wait_ge(ready["stat"], 4 * UNITS)
            for h in range(2):
                sp.wait_ge(x3_stored[h], 16 * UNITS)
                sp.wait_ge(hpre_stored[h], 16 * UNITS)
            for i in range(EARLY_PARTS, parts):
                load_back(hpre_dram, i, hpre_late)
            for i in range(parts):
                sp.wait_ge(relu_ready, 2 * (i + 1) * q)
                load_back(x3_dram, i, x3_back)

            def store(g, r):
                wait_fin(sp, g, r)
                sp.dma_start(out[g], fin[:, r]).then_inc(stored[r], 16)

            ring(sp, store)
            for r in range(RING):
                sp.wait_ge(stored[r], 16 * (GROUPS // RING))

        @block.gpsimd
        def _(pool):
            pool.memset(eps4[:], EPS).then_inc(setup_pool, 1)
            pool.memset(mhalf[:], -0.5).then_inc(setup_pool, 1)
            pool.memset(ones[:], 1.0).then_inc(setup_pool, 1)
            pool.memset(mone[:], -1.0).then_inc(setup_pool, 1)
            pool.wait_ge(setup_pool, 4)
            pool.wait_ge(setup_dve, 7)
            pool.tensor_tensor(dinv[:], deg[:, 3:4], mhalf[:, 0:1], ALU.pow).then_inc(setup_pool, 1)

            def make_rstd(n, h, count):
                pool.wait_ge(aggregated[n], count)
                pool.tensor_tensor(lnve[:, n, h, :], lnmv[:, n, h, :, 1], eps4[:], ALU.add).then_inc(eps_added[n], 1)
                pool.wait_ge(eps_added[n], count)
                pool.tensor_tensor(lnr[:, n, h, :], lnve[:, n, h, :], mhalf[:], ALU.pow).then_inc(rstd[n], 1)

            def body(t):
                for step, h in ORDER:
                    if not present(step, t):
                        continue
                    if step == "stats1":
                        make_rstd(0, h, half_number(step, t, h) + 1)
                    if step == "stats2":
                        make_rstd(1, h, half_number(step, t, h) + 1)
                    if step == "stats3":
                        make_rstd(2, h, half_number(step, t, h) + 1)
                    if step == "norm1":
                        n = half_number(step, t, h)
                        if isinstance(t, int) and t == 0:
                            pool.wait_ge(split_hi, len(SPLITS))
                            pool.wait_ge(split_lo, len(SPLITS))
                        pool.wait_ge(setup_pool, 5)
                        pool.wait_ge(ready["x1"], n + 1)
                        pool.tensor_copy(AGG[:, n, :],
                                         x1[:, h].rearrange("p b d -> p (b d)")).then_inc(ready["x1_kept"], 1)

            bodies(pool, body)

            pool.wait_ge(bn_dve, 3)
            pool.tensor_tensor(bn[:, 4:6], bn[:, 2:4], mhalf[:, 0:2], ALU.pow).then_inc(bn_pool, 1)
            pool.wait_ge(bn_dve, 10)
            pool.tensor_tensor(bn[:, 12:13], bn[:, 11:12], mhalf[:, 0:1], ALU.pow).then_inc(bn_pool, 1)

            def fin_rstd(g, r):
                pool.wait_ge(f_mv, g + 1)
                pool.tensor_tensor(fve[:, r, :], fmv[:, r, :, 1], eps4[:], ALU.add)
                pool.tensor_tensor(fnm[:, r, :], fmv[:, r, :, 0], mone[:], ALU.mult).then_inc(f_eps, 1)
                pool.wait_ge(f_eps, g + 1)
                pool.tensor_tensor(frs[:, r, :], fve[:, r, :], mhalf[:], ALU.pow).then_inc(f_pow, 1)
                pool.wait_ge(f_pow, g + 1)
                pool.tensor_tensor(fnb[:, r, :], fnm[:, r, :], frs[:, r, :], ALU.mult).then_inc(f_rstd, 1)

            ring(pool, fin_rstd, TAIL)

        @block.tensor
        def _(pe):
            mm = pe.matmul
            pe.wait_ge(setup_dve, 1)

            def setup_products():
                pe.wait_ge(loaded_first, NFIRST)
                pe.wait_ge(setup_pool, 4)
                mm(G[0:1, 0, 0:N], ones[:, 0:1], AT[:], start=True, stop=True).then_inc(setup_pe, 1)
                mm(G[:, 1, 0:128], a12[:, 0:1].to_broadcast([128, 128]), w_l2T[:],
                   start=True, stop=True).then_inc(setup_pe, 1)
                mm(G[:, 2, 0:128], w_l2T[:], a12[:, 1:2].to_broadcast([128, 128]),
                   start=True, stop=True).then_inc(setup_pe, 1)
                pe.wait_ge(setup_dve, 8)
                mm(G[:, 3, 0:N], ones[:], scratch[:], start=True, stop=True).then_inc(setup_pe, 1)

            def fill(step, h, t, j=0):
                f = (step, h, j)
                before = fill_before(f, t)
                if before:
                    pe.wait_ge(*read_signal(*before))
                return F[:, BANK[f], :]

            def full(step, h, j=0):
                return filled[BANK[(step, h, j)]]

            def fused_step(step, h, t):
                n = half_number(step, t, h) if step not in ("inputs", "gates") else None
                if step == "ax":
                    pe.wait_ge(x_loaded[h], (t - LAG[step]) * 16 + 16)
                    o = per_batch(fill(step, h, t))
                    for b in range(BH):
                        i = mm(o[:, b, :], xin[:, h, b, :], A2T[:], start=True, stop=True)
                    i.then_inc(full(step, h), 1)
                if step == "h1":
                    pe.wait_ge(ready["yT"], n + 1)
                    if isinstance(t, int) and t == 0:
                        pe.wait_ge(loaded_first, NFIRST)
                    for j in range(2):
                        o = fill(step, h, t, j).rearrange("p (b f) -> p b f", b=2)
                        for b in range(2):
                            i = mm(o[:, b, :], yT[:, h, 2 * j + b, :], w1[:], start=True, stop=True)
                        i.then_inc(full(step, h, j), 1)
                if step == "ah1":
                    pe.wait_ge(ready["h1_0"], n + 1)
                    pe.wait_ge(ready["h1_1"], n + 1)
                    for k in range(2):
                        o = per_batch(fill(step, h, t, k))
                        for b in range(BH):
                            i = mm(o[:, b, :], h1[:, h, b, k * 128:(k + 1) * 128], A2T[:], start=True, stop=True)
                        i.then_inc(full(step, h, k), 1)
                if step in ("h2a", "h2b"):
                    if isinstance(t, int) and t == 0:
                        pe.wait_ge(split_lo, 2)
                    for j in range(2):
                        c = j + 2 * (step == "h2b")
                        o = per_batch(fill(step, h, t, j))
                        for k in range(2):
                            if c == 0:
                                pe.wait_ge(ready[f"y2T_{k}"], n + 1)
                            for a, d in PASSES:
                                i = mm(o, w2[:, a, k, c * 128:(c + 1) * 128], y2T[:, d, k],
                                       start=(k == 0 and a == d), stop=(k == 1 and (a, d) == PASSES[-1]))
                        i.then_inc(full(step, h, j), 1)
                if step == "z":
                    if isinstance(t, int) and t == 0:
                        pe.wait_ge(loaded, NLOAD)
                    o = per_batch(fill(step, h, t))
                    for c in range(4):
                        pe.wait_ge(ready[f"h2T_{c}"], n + 1)
                    for b in range(BH):
                        for c in range(4):
                            i = mm(o[:, b, :], h2T[:, c, b, :], w3[:, c, :], start=(c == 0), stop=(c == 3))
                    i.then_inc(full(step, h), 1)
                if step == "oz":
                    pe.wait_ge(ready["z"], n + 1)
                    mm(per_batch(fill(step, h, t)), A2T[:], z[:, h], start=True, stop=True)\
                        .then_inc(full(step, h), 1)
                if step == "gax":
                    pe.wait_ge(ready["x1"], n + 1)
                    o = per_batch(fill(step, h, t))
                    for b in range(BH):
                        i = mm(o[:, b, :], x1[:, h, b, :], AT[:], start=True, stop=True)
                    i.then_inc(full(step, h), 1)
                if step == "gh":
                    pe.wait_ge(ready["gyT"], n + 1)
                    o = per_batch(fill(step, h, t))
                    if isinstance(t, int) and t == 0:
                        pe.wait_ge(rows_built, 16 * 4 * 2)
                    mm(o, rs4[:, 0, :], bg4[:, 0:1, :].to_broadcast([4, BH, D]), start=True, stop=False,
                       skip_group_check=True)
                    for b in range(BH):
                        i = mm(o[:, b, :], yT[:, h, b, :], wg0[:], start=False, stop=(b == BH - 1),
                               skip_group_check=True)
                    i.then_inc(full(step, h), 1)
                if step == "gah":
                    pe.wait_ge(ready["gh1"], n + 1)
                    o = per_batch(fill(step, h, t))
                    for b in range(BH):
                        i = mm(o[:, b, :], h1[:, h, b, 0:D], AT[:], start=True, stop=True)
                    i.then_inc(full(step, h), 1)
                if step == "gx":
                    pe.wait_ge(ready["gy2T"], n + 1)
                    o = per_batch(fill(step, h, t))
                    mm(o, bg4[:, 1, :], rs4[:].to_broadcast([4, BH, N]), start=True, stop=False)
                    if isinstance(t, int) and t == 0:
                        pe.wait_ge(split_lo, 3)
                    for a, d in PASSES:
                        i = mm(o, wg1[:, a, :], gah_parts(h)[d], start=False, stop=(a, d) == PASSES[-1])
                    i.then_inc(full(step, h), 1)
                if step == "inputs":
                    lstm_inputs(h, t)
                if step == "gates":
                    lstm_gates(h, t)
                if step == "backT":
                    pe.wait_ge(h_ready, (t - LAG[step]) * NSLOT + NSLOT)
                    o = per_batch(fill(step, h, t))
                    for b in range(BH):
                        for d in (HI, LO):
                            i = mm(o[:, b, :], HT[:, d, BH * h + b, :], I_r[:], start=(d == HI), stop=(d == LO))
                    i.then_inc(full(step, h), 1)
                if step == "x2T":
                    pe.wait_ge(ready["x2"], n + 1)
                    o = per_batch(fill(step, h, t))
                    for b in range(BH):
                        i = pe.transpose(o[:, b, :], x2[:, h, b, :], I_[:])
                    i.then_inc(full(step, h), 1)
                if step == "wh":
                    pe.wait_ge(ready["x2T"], n + 1)
                    o = per_batch(fill(step, h, t))
                    for b in range(BH):
                        i = mm(o[:, b, :], x2T[:, h, b, :], w_l2[:], start=True, stop=True)
                    i.then_inc(full(step, h), 1)
                if step == "s2":
                    mm(per_batch(fill(step, h, t)), wa2[:], x2T[:, h], start=True, stop=True)\
                        .then_inc(full(step, h), 1)
                if step == "pT":
                    pe.wait_ge(ready["P"], n + 1)
                    o = per_batch(fill(step, h, t))
                    for b in range(BH):
                        i = pe.transpose(o[:, b, :], E[:, h, b, :], I_[:])
                    i.then_inc(full(step, h), 1)
                if step == "att":
                    pe.wait_ge(ready["PT"], n + 1)
                    pe.wait_ge(ready["wh"], n + 1)
                    o = per_batch(fill(step, h, t))
                    for b in range(BH):
                        i = mm(o[:, b, :], x2T[:, h, b, :], wh[:, h, b, :], start=True, stop=True)
                    i.then_inc(full(step, h), 1)
                if step == "agg":
                    pe.wait_ge(ready["x3"], n + 1)
                    o = per_batch(fill(step, h, t))
                    for b in range(BH):
                        i = mm(o[:, b, :], x2[:, h, b, :], AHT[:], start=True, stop=True)
                    i.then_inc(full(step, h), 1)
                if step == "stat":
                    pe.wait_ge(ready["agg"], n + 1)
                    for k in range(2):
                        o = per_batch(fill(step, h, t, k))
                        for a, d in PASSES:
                            i = mm(o, w1T_l3[:, a, k * 128:(k + 1) * 128], agg_parts(h, n)[d],
                                   start=(a == d), stop=(a, d) == PASSES[-1])
                        i.then_inc(full(step, h, k), 1)

            def gate_products(s, g, weights, data, passes, first, last):
                p, _, _, nb = SLOTS[s]
                o = G[:, g, 0:nb * (N // p)].rearrange("p (b w) -> p b w", b=nb)
                for a, d in passes:
                    i = mm(o, weights[:, a, g * D:(g + 1) * D], data[d], start=first and (a, d) == PASSES[0],
                           stop=last and (a, d) == PASSES[-1], skip_group_check=True)
                return i

            def slot_operands(s):
                p, step, b0, nb = SLOTS[s]
                nw = N // p
                if p == 1:
                    return [xl[:, d, b0:b0 + nb, :] for d in (HI, LO)], wih[:, :, p - 1, :], None, None
                src = [HT[:, d, :, step:step + (nw - 1) * p + 1:p] for d in (HI, LO)]
                inner = [hs[:, d, 0:nb * nw].rearrange("p (b w) -> p b w", b=nb) for d in (HI, LO)]
                return src, wih[:, :, p - 1, :], inner, (whh[:, :, p - 2, :] if step else None)

            def lstm_inputs(s, t):
                src, w_in, _, _ = slot_operands(s)
                pe.wait_ge(cell_ready, (t - LAG["inputs"]) * NSLOT + s)
                for g in (GATE_I, GATE_G, GATE_F):
                    gate_products(s, g, w_in, src, PASSES, True, False)

            def lstm_gates(s, t):
                p, step, b0, nb = SLOTS[s]
                unit = t - LAG["gates"]
                if isinstance(t, int) and unit == 0 and s == 0:
                    pe.wait_ge(split_lo, len(SPLITS))
                src, w_in, inner, w_h = slot_operands(s)
                before = unit * NSLOT + s
                if p == 1:
                    pe.wait_ge(ready["xl"], unit * 2 + b0 // BH + 1)
                    wait(pe, cell_ready, before)
                    for g in (GATE_I, GATE_G):
                        gate_products(s, g, w_in, src, PASSES, True, True).then_inc(gates_filled, 1)
                    wait(pe, h_made, before)
                    gate_products(s, GATE_O, w_in, src, PASSES, True, True).then_inc(gates_filled, 1)
                    return
                data, w = (inner, w_h) if step else (src, w_in)
                pe.wait_ge(h_hi, before)
                for g in (GATE_I, GATE_G):
                    gate_products(s, g, w, data, PASSES[:2], not step, False)
                pe.wait_ge(h_ready, before)
                for g in (GATE_I, GATE_G):
                    gate_products(s, g, w, data, PASSES[2:], not step, True).then_inc(gates_filled, 1)
                if step:
                    gate_products(s, GATE_F, w, data, PASSES, False, True).then_inc(gates_filled, 1)
                    gate_products(s, GATE_O, w_in, src, PASSES, True, False)
                gate_products(s, GATE_O, w, data, PASSES, not step, True).then_inc(gates_filled, 1)

            def body(t):
                for step, h in ORDER:
                    if present(step, t):
                        fused_step(step, h, t)
                    if isinstance(t, int) and t == 0 and (step, h) == ("h1", 1):
                        setup_products()

            bodies(pe, body)

            def features(g, r):
                wait(pe, out_kept, late(g, g - RING + 1))
                for k in range(2):
                    pe.wait_ge(relu_ready, g * 2 + k + 1)
                    i = mm(F[:, r, :], w2T_l3[:, k, :], relu[:, r, k, :], start=(k == 0), stop=(k == 1))
                i.then_inc(out_filled, 1)

            ring(pe, features)

            def rows(g, r):
                wait_fin(pe, g, r, TAIL)
                mm(tail_bank(r), I_[:], X3[:, g, :], start=True, stop=False, skip_group_check=True)
                o = per_batch(tail_bank(r))
                pe.wait_ge(affine_ready, g + 1)
                for b in range(BH):
                    i = mm(o[:, b, :], oaff[:, r % RING, b * N:(b + 1) * N], I_[:], start=False, stop=(b == BH - 1),
                           skip_group_check=True)
                i.then_inc(rows_filled, 1)

            pe.wait_ge(out_kept, GROUPS)
            pe.wait_ge(x3_back, 16 * 8)
            ring(pe, rows, TAIL)

        @block.scalar
        def _(act):
            def take(step, h, t, dst, name, func=ACT.Copy, j=0):
                wait_filled(act, step, h, t, j)
                act.activation(dst, bank_of(step, h, j).rearrange("p (b n) -> p b n", b=dst.shape[1]),
                               func).then_inc(ready[name], 1)

            def fused_step(step, h, t):
                n = half_number(step, t, h)
                if step == "wh":
                    act.wait_ge(ready["s1"], n + 1)
                for j in moves(step, SCALAR_MOVES):
                    dst, name, relu_ = moved(step, h, n, j)
                    take(step, h, t, dst, name, ACT.Relu if relu_ else ACT.Copy, j)
                if step == "ah1":
                    for k in range(2):
                        take(step, h, t, y2T[:, HI, k], f"y2T_hi{k}", ACT.Copy, k)
                if step == "gah":
                    take(step, h, t, gah_parts(h)[HI], "gy2T_hi")
                if step == "agg":
                    act.wait_ge(setup_dve, SETUP_STEPS)
                    take(step, h, t, agg_parts(h, n)[HI], "agg_hi")
                if step == "gx":
                    take(step, h, t, xl[:, HI, BH * h:BH * h + BH, :], "xl_hi", ACT.Relu)
                if step == "stat":
                    for k, dst in enumerate((E[:, h], per_batch(AGG[:, n, :]))):
                        act.wait_ge(setup_dve, SETUP_STEPS)
                        wait_filled(act, step, h, t, k)
                        act.activation(dst, per_batch(bank_of(step, h, k)), ACT.Copy).then_inc(ready["hpre"], 1)
                if step == "expo":
                    act.wait_ge(ready["nmax"], n + 1)
                    for b in range(BH):
                        i = act.activation(E[:, h, b, :], E[:, h, b, :], ACT.Exp, bias=nmax[:, h, b:b + 1],
                                           accum_out=psum_[:, h, b:b + 1])
                    i.then_inc(ready["P"], 1)
                if step == "gates":
                    if isinstance(t, int) and t == LAG[step] and h == 0:
                        act.wait_ge(bias_ready, 2)
                    p, _, _, nb = SLOTS[h]
                    width = nb * (N // p)
                    unit = t - LAG[step]
                    for i, g in enumerate(slot_gates(h)):
                        act.wait_ge(gates_filled, unit * GATES_BEFORE[NSLOT] + GATES_BEFORE[h] + i + 1)
                        act.activation(gact[:, 0:width] if g == GATE_G else G[:, g, 0:width],
                                       G[:, g, 0:width], ACT.Tanh,
                                       bias=gbias[:, p - 1, g:g + 1], scale=1.0 if g == GATE_G else 0.5)\
                            .then_inc(gates_done, 1)
                if step == "tanhc":
                    p, _, _, nb = SLOTS[h]
                    width = nb * (N // p)
                    act.wait_ge(cell_ready, (t - LAG[step]) * NSLOT + h + 1)
                    act.activation(tanhc[:, 0:width], cell[:, 0:width], ACT.Tanh, scale=0.5)\
                        .then_inc(tanhc_ready, 1)

            def body(t):
                for step, h in ORDER:
                    if present(step, t):
                        fused_step(step, h, t)
                    if isinstance(t, int) and t == 0 and (step, h) == ("h1", 1):
                        act.wait_ge(loaded_second, 16 * len(SECOND_LOADS))
                        split_weights(SPLITS[:3])
                    if isinstance(t, int) and t == 0 and (step, h) == ("h2b", 0):
                        act.wait_ge(loaded, NLOAD)
                        split_weights(SPLITS[3:])

            def split_weights(some):
                for raw, parts, factor in some:
                    act.activation(parts[:, HI, :], raw, ACT.Copy, scale=factor).then_inc(split_hi, 1)

            bodies(act, body)

            act.wait_ge(bn_dve, 6)
            for h in range(2):
                act.wait_ge(x3_stored[h], 16 * UNITS)

            def relu_group(g, r):
                wait(act, out_filled, late(g, g - RING + 1))
                if isinstance(g, int) and g == PEEL - 1:
                    act.wait_ge(hpre_late, 16 * (8 - EARLY_PARTS))
                for k, src in enumerate((X3, AGG)):
                    act.activation(relu[:, r, k, :], src[:, g, :], ACT.Relu, bias=bn[:, 6 + k:7 + k],
                                   scale=bn[:, 8 + k:9 + k]).then_inc(relu_ready, 1)

            act.wait_ge(hpre_early, 16 * EARLY_PARTS)
            ring(act, relu_group)

            def affine(g, r):
                wait(act, rows_filled, late(g, g - RING + 1))
                act.activation(oaff[:, r % RING, :], AGG[:, g, :], ACT.Identity, bias=bn[:, 14:15],
                               scale=bn[:, 13:14]).then_inc(affine_ready, 1)

            def finish(g, r):
                act.wait_ge(f_rstd, g + 1)
                if not isinstance(g, int) or g >= RING:
                    act.wait_ge(stored[r % RING], (g - r % RING) * (16 // RING))
                o = per_batch(tail_bank(r))
                for b in range(BH):
                    i = act.activation(fin[:, r % RING, b, :], o[:, b, :], ACT.Identity, bias=fnb[:, r, b:b + 1],
                                       scale=frs[:, r, b:b + 1])
                i.then_inc(fin_ready[r % RING], 4)

            def one(g, r):
                affine(g, r)
                if (r - BEHIND) % RING != VECTOR_PLACE and (not isinstance(g, int) or g >= BEHIND):
                    finish(g - BEHIND, (r - BEHIND) % TAIL)

            act.wait_ge(bn_dve, 13)
            ring(act, one, TAIL)
            for g in range(GROUPS - BEHIND, GROUPS):
                if g % RING != VECTOR_PLACE:
                    finish(g, g % TAIL)

        @block.vector
        def _(dve):
            setup = [0]

            def chain(i):
                setup[0] += 1
                i.then_inc(setup_dve, 1)
                dve.wait_ge(setup_dve, setup[0])

            dve.wait_ge(adjT_loaded, 16)
            chain(V.tensor_tensor(A2T[:], AT[:], AT[:], ALU.mult))
            dve.wait_ge(loaded_first, NFIRST)
            dve.wait_ge(setup_pool, 4)
            chain(V.tensor_scalar(maskadd[:], A_[:], 0.0, MASKED, ALU.is_equal, ALU.mult))
            V.tensor_tensor(ANT[:], AT[:], I_[:], ALU.add)
            chain(V.tensor_tensor(A_[:], A_[:], I_[:], ALU.add))
            chain(V.tensor_tensor(scratch[:], A_[:], I_[:], ALU.mult))
            for k, m in enumerate((ANT, A_, scratch)):
                i = V.tensor_reduce(deg[:, k:k + 1], m[:], axis=AX.X, op=ALU.add)
            chain(i)
            chain(V.tensor_tensor(deg[:, 3:4], deg[:, 0:1], deg[:, 1:2], ALU.add))
            chain(V.tensor_tensor(deg[:, 3:4], deg[:, 3:4], deg[:, 2:3], ALU.subtract))
            dve.wait_ge(setup_pool, 5)
            V.tensor_scalar(AHT[:], ANT[:], dinv[:], None, ALU.mult)
            chain(V.tensor_scalar(scratch[:], I_[:], dinv[:], None, ALU.mult))
            dve.wait_ge(setup_pe, 4)
            chain(V.tensor_tensor(AHT[:], G[:, 3, 0:N], AHT[:], ALU.mult))
            V.tensor_copy(rs_hl[:, HI, :], G[0:1, 0, 0:N])
            V.tensor_copy(bg_hl[:, :, HI, :], bg[:])
            V.tensor_copy(wa1[:], G[:, 1, 0:128])
            V.tensor_copy(I_r[:], I_[:])
            chain(V.tensor_copy(wa2[:], G[:, 2, 0:128]))
            V.tensor_tensor(rs_hl[:, LO, :], G[0:1, 0, 0:N], rs_hl[:, HI, :].bitcast(fp32), ALU.subtract)
            chain(V.tensor_tensor(bg_hl[:, :, LO, :], bg[:], bg_hl[:, :, HI, :].bitcast(fp32),
                                  ALU.subtract))

            biases = [0]

            def bias_chain(i):
                biases[0] += 1
                i.then_inc(bias_ready, 1)
                dve.wait_ge(bias_ready, biases[0])

            def split_weights(parts_of):
                for n in parts_of:
                    raw, parts, factor = SPLITS[n]
                    dve.wait_ge(split_hi, n + 1)
                    V.scalar_tensor_tensor(parts[:, LO, :], raw, factor, parts[:, HI, :].bitcast(fp32), ALU.mult,
                                           ALU.subtract).then_inc(split_lo, 1)

            def lstm_biases():
                dve.wait_ge(loaded, NLOAD)
                bias_chain(V.tensor_tensor(gbias[:], gbias[:], bhh[:], ALU.add))
                for g in (GATE_I, GATE_F, GATE_O):
                    i = V.tensor_scalar(gbias[:, :, g], gbias[:, :, g], 0.5, None, ALU.mult)
                bias_chain(i)

            def take(step, h, t, dst, name, j, relu_):
                wait_filled(dve, step, h, t, j)
                src = bank_of(step, h, j).rearrange("p (b n) -> p b n", b=dst.shape[1])
                if relu_:
                    i = V.tensor_scalar(dst, src, 0.0, None, ALU.max)
                else:
                    i = V.tensor_copy(dst, src)
                i.then_inc(ready[name], 1)

            def stats(n, h, r, count):
                dve.wait_ge(added[n], count)
                for b in range(BH):
                    i = V.bn_stats(lnst[:, n, h, b, :], r[:, b, :])
                i.then_inc(stated[n], 1)
                dve.wait_ge(stated[n], count)
                V.tensor_copy(carry[:], lnst[:, n, h, 0, 0:1])
                for b in range(BH):
                    i = V.bn_aggr(lnmv[:, n, h, b, :], lnst[:, n, h, b, :])
                i.then_inc(aggregated[n], 1)

            def normalise(n, h, r, name, count):
                dve.wait_ge(rstd[n], count)
                for b in range(BH):
                    i = V.tensor_scalar(r[:, b, :], r[:, b, :], lnmv[:, n, h, b, 0:1], lnr[:, n, h, b:b + 1],
                                        ALU.subtract, ALU.mult)
                i.then_inc(ready[name], 1)

            def fused_step(step, h, t):
                lstm = step in ("gates", "tanhc", "hout")
                n = None if lstm else half_number(step, t, h)
                if step == "ah1":
                    for k in range(2):
                        dve.wait_ge(ready[f"y2T_hi{k}"], n + 1)
                        V.tensor_tensor(y2T[:, LO, k], per_batch(bank_of(step, h, k)),
                                        y2T[:, HI, k].bitcast(fp32), ALU.subtract).then_inc(ready[f"y2T_{k}"], 1)
                if step in ("gah", "agg"):
                    name = "gy2T" if step == "gah" else "agg"
                    hi, lo = gah_parts(h) if step == "gah" else agg_parts(h, n)
                    dve.wait_ge(ready[name + "_hi"], n + 1)
                    V.tensor_tensor(lo, per_batch(bank_of(step, h)), hi.bitcast(fp32), ALU.subtract)\
                        .then_inc(ready[name], 1)
                if step == "gx":
                    part = xl[:, :, BH * h:BH * h + BH, :]
                    dve.wait_ge(ready["xl_hi"], n + 1)
                    V.scalar_tensor_tensor(part[:, LO].rearrange("p b n -> p (b n)"), bank_of(step, h), 0.0,
                                           part[:, HI].bitcast(fp32).rearrange("p b n -> p (b n)"),
                                           ALU.max, ALU.subtract).then_inc(ready["xl"], 1)
                if step == "oz":
                    if not isinstance(t, int) or t > 0:
                        dve.wait_ge(ready["x1_kept"], n - 1)
                    wait_filled(dve, step, h, t)
                    V.tensor_tensor(x1[:, h], per_batch(bank_of(step, h)), xin[:, h], ALU.add)\
                        .then_inc(added[0], 1)
                for k, r in enumerate((x1, x2, x2)):
                    if step == f"stats{k + 1}":
                        stats(k, h, r[:, h], n + 1)
                if step == "norm1":
                    normalise(0, h, x1[:, h], "x1", n + 1)
                if step == "backT":
                    wait_filled(dve, step, h, t)
                    dve.wait_ge(ready["x1_kept"], n + 1)
                    if not isinstance(t, int) or t > LAG[step]:
                        dve.wait_ge(x3_stored[h], (t - LAG[step]) * 16)
                    V.scalar_tensor_tensor(x2[:, h].rearrange("p b d -> p (b d)"), bank_of(step, h), 0.5,
                                           AGG[:, n, :], ALU.mult, ALU.add).then_inc(added[1], 1)
                if step == "norm2":
                    normalise(1, h, x2[:, h], "x2", n + 1)
                if step == "s1":
                    dve.wait_ge(ready["x2"], n + 1)
                    for b in range(BH):
                        i = V.scalar_tensor_tensor(wh[:, h, b, :], x2[:, h, b, :], 1.0, wa1[:], ALU.mult, ALU.mult,
                                                   accum_out=s1[:, BH * h + b:BH * h + b + 1])
                    i.then_inc(ready["s1"], 1)
                if step == "wh":
                    dve.wait_ge(ready["s1"], n + 1)
                for j in moves(step, VECTOR_MOVES):
                    take(step, h, t, *moved(step, h, n, j)[:2], j, moved(step, h, n, j)[2])
                if step == "s2":
                    wait_filled(dve, step, h, t)
                    dve.wait_ge(ready["s1"], n + 1)
                    if not isinstance(t, int) or t > LAG[step]:
                        dve.wait_ge(hpre_stored[h], (t - LAG[step]) * 16)
                    o = per_batch(bank_of(step, h))
                    for b in range(BH):
                        i = V.scalar_tensor_tensor(E[:, h, b, :], o[:, b, :], s1[:, BH * h + b:BH * h + b + 1],
                                                   maskadd[:], ALU.add, ALU.add)
                    i.then_inc(ready["E"], 1)
                if step == "lrelu":
                    dve.wait_ge(ready["E"], n + 1)
                    V.scalar_tensor_tensor(E[:, h], E[:, h], ALPHA, E[:, h], ALU.mult, ALU.max)\
                        .then_inc(ready["L"], 1)
                if step == "rowmax":
                    dve.wait_ge(ready["L"], n + 1)
                    V.tensor_reduce(nmax[:, h], E[:, h], axis=AX.X, op=ALU.max, negate=True)\
                        .then_inc(ready["nmax"], 1)
                if step == "pT":
                    dve.wait_ge(ready["P"], n + 1)
                    V.reciprocal(rsum[:, h], psum_[:, h]).then_inc(ready["rsum"], 1)
                if step == "att":
                    wait_filled(dve, step, h, t)
                    dve.wait_ge(ready["rsum"], n + 1)
                    o = per_batch(bank_of(step, h))
                    for b in range(BH):
                        i = V.scalar_tensor_tensor(x2[:, h, b, :], o[:, b, :], rsum[:, h, b:b + 1],
                                                   x2[:, h, b, :], ALU.mult, ALU.add)
                    i.then_inc(added[2], 1)
                if step == "norm3":
                    normalise(2, h, x2[:, h], "x3", n + 1)
                if step == "stat":
                    for k in range(2):
                        dve.wait_ge(setup_dve, SETUP_STEPS)
                        dve.wait_ge(ready["hpre"], 2 * n + k + 1)
                        V.bn_stats(stats1[:, k, n, :], AGG[:, n, :] if k else
                                   E[:, h].rearrange("p b n -> p (b n)")).then_inc(ready["stat"], 1)
                if step == "gates":
                    p, later, _, nb = SLOTS[h]
                    w = nb * (N // p)
                    unit = t - LAG[step]
                    done = unit * GATES_BEFORE[NSLOT] + GATES_BEFORE[h]
                    dve.wait_ge(gates_done, done + 2)
                    if not later:
                        V.scalar_tensor_tensor(cell[:, 0:w], G[:, GATE_I, 0:w], 1.0, gact[:, 0:w],
                                               ALU.add, ALU.mult).then_inc(cell_ready, 1)
                    else:
                        V.scalar_tensor_tensor(gact[:, 0:w], G[:, GATE_I, 0:w], 1.0, gact[:, 0:w],
                                               ALU.add, ALU.mult).then_inc(terms_done, 1)
                        dve.wait_ge(gates_done, done + 3)
                        V.scalar_tensor_tensor(cell[:, 0:w], G[:, GATE_F, 0:w], 1.0, cell[:, 0:w],
                                               ALU.add, ALU.mult).then_inc(terms_done, 1)
                        dve.wait_ge(terms_done, unit * 2 * LATER_BEFORE[NSLOT] + 2 * LATER_BEFORE[h] + 2)
                        V.scalar_tensor_tensor(cell[:, 0:w], cell[:, 0:w], 0.5, gact[:, 0:w],
                                               ALU.mult, ALU.add).then_inc(cell_ready, 1)
                if step == "hout":
                    p, _, _, nb = SLOTS[h]
                    w = nb * (N // p)
                    unit = t - LAG[step]
                    src, dst = h_views(h)
                    o_gate = G[:, GATE_O, 0:w].rearrange("p (b w) -> p b w", b=nb)
                    tanh_c = tanhc[:, 0:w].rearrange("p (b w) -> p b w", b=nb)
                    dve.wait_ge(tanhc_ready, unit * NSLOT + h + 1)
                    if h == 0:
                        V.scalar_tensor_tensor(src, o_gate, 1.0, tanh_c, ALU.add, ALU.mult).then_inc(h_made, 1)
                        dve.wait_ge(h_made, unit * NSLOT + 1)
                        V.tensor_copy(dst[HI], src).then_inc(h_hi, 1)
                    else:
                        V.scalar_tensor_tensor(dst[HI], o_gate, 1.0, tanh_c, ALU.add, ALU.mult).then_inc(h_hi, 1)
                        V.scalar_tensor_tensor(src, o_gate, 1.0, tanh_c, ALU.add, ALU.mult).then_inc(h_made, 1)
                        dve.wait_ge(h_made, unit * NSLOT + h + 1)
                    dve.wait_ge(h_hi, unit * NSLOT + h + 1)
                    V.tensor_tensor(dst[LO], src, dst[HI].bitcast(fp32), ALU.subtract).then_inc(h_ready, 1)

            def body(t):
                for step, h in ORDER:
                    if present(step, t):
                        fused_step(step, h, t)
                    if isinstance(t, int) and t == 0 and (step, h) == ("h1", 1):
                        split_weights(range(3))
                    if isinstance(t, int) and t == 0 and (step, h) == ("h2b", 1):
                        split_weights(range(3, len(SPLITS)))
                        lstm_biases()

            bodies(dve, body)

            bns = [0]

            def bn_chain(i):
                bns[0] += 1
                i.then_inc(bn_dve, 1)
                dve.wait_ge(bn_dve, bns[0])

            dve.wait_ge(ready["stat"], 4 * UNITS)
            mv = scratch[:, 0:4].rearrange("p (k c) -> p k c", k=2)
            for k in range(2):
                i = V.bn_aggr(mv[:, k, :], stats1[:, k].rearrange("p g s -> p (g s)"))
            bn_chain(i)
            bn_chain(V.tensor_tensor(bn[:, 0:2], mv[:, :, 0], vec1[:, 0, :], ALU.add))
            bn_chain(V.tensor_scalar(bn[:, 2:4], mv[:, :, 1], EPS, None, ALU.add))
            dve.wait_ge(bn_pool, 1)
            bn_chain(V.tensor_tensor(bn[:, 8:10], bn[:, 4:6], vec1[:, 1, :], ALU.mult))
            bn_chain(V.tensor_tensor(bn[:, 0:2], vec1[:, 0, :], bn[:, 0:2], ALU.subtract))
            V.tensor_tensor(bn[:, 0:2], bn[:, 0:2], bn[:, 8:10], ALU.mult).then_inc(shift_term, 1)
            dve.wait_ge(shift_term, 1)
            bn_chain(V.tensor_tensor(bn[:, 6:8], bn[:, 0:2], vec1[:, 2, :], ALU.add))

            def keep(g, r):
                dve.wait_ge(out_filled, g + 1)
                V.tensor_scalar(AGG[:, g, :], F[:, r, :], 1.0, None, ALU.mult)
                V.bn_stats(stats2[:, g, :], F[:, r, :]).then_inc(out_kept, 1)

            ring(dve, keep)

            dve.wait_ge(out_kept, GROUPS)
            bn_chain(V.bn_aggr(scratch[:, 8:10], stats2[:].rearrange("p g s -> p (g s)")))
            bn_chain(V.tensor_tensor(bn[:, 10:11], scratch[:, 8:9], vec2[:, 0, :], ALU.add))
            bn_chain(V.tensor_tensor(bn[:, 10:11], vec2[:, 0, :], bn[:, 10:11], ALU.subtract))
            bn_chain(V.tensor_scalar(bn[:, 11:12], scratch[:, 9:10], EPS, None, ALU.add))
            dve.wait_ge(bn_pool, 2)
            bn_chain(V.tensor_tensor(bn[:, 13:14], bn[:, 12:13], vec2[:, 1, :], ALU.mult))
            bn_chain(V.tensor_tensor(bn[:, 10:11], bn[:, 10:11], bn[:, 13:14], ALU.mult))
            bn_chain(V.tensor_tensor(bn[:, 14:15], bn[:, 10:11], vec2[:, 2, :], ALU.add))

            def statistics(g, r):
                dve.wait_ge(rows_filled, g + 1)
                o = per_batch(tail_bank(r))
                for b in range(BH):
                    i = V.bn_stats(fst[:, r, b, :], o[:, b, :])
                i.then_inc(f_stats, 1)
                dve.wait_ge(f_stats, g + 1)
                V.tensor_copy(carry[:], fst[:, r, 0, 0:1])
                for b in range(BH):
                    i = V.bn_aggr(fmv[:, r, b, :], fst[:, r, b, :])
                i.then_inc(f_mv, 1)

            def finish(g, r):
                dve.wait_ge(f_rstd, g + 1)
                if not isinstance(g, int) or g >= RING:
                    dve.wait_ge(stored[r % RING], (g - r % RING) * (16 // RING))
                o = per_batch(tail_bank(r))
                for b in range(BH):
                    i = V.tensor_scalar(fin[:, r % RING, b, :], o[:, b, :], fmv[:, r, b, 0:1], frs[:, r, b:b + 1],
                                        ALU.subtract, ALU.mult)
                i.then_inc(fin_ready[r % RING], 4)

            def one(g, r):
                statistics(g, r)
                if (r - 2) % RING == VECTOR_PLACE and (not isinstance(g, int) or g >= 2):
                    finish(g - 2, (r - 2) % TAIL)

            ring(dve, one, TAIL)
            finish(GROUPS - 1, TAIL - 1)


def kernel(**inputs):
    import numpy as np
    import concourse.bacc as bacc
    from concourse import mybir as mb
    from concourse.bass_utils import run_bass_kernel_spmd as run

    i = {k: np.asarray(v) for k, v in inputs.items()}
    cols = lambda a, k: a.reshape(k, 128).T
    data = {
        "x": i["x"].reshape(GROUPS, BH, N, D).transpose(0, 2, 1, 3).reshape(GROUPS, N, BH, D),
        "adj": i["adj"], "adjT": i["adj"].T,
        "l0_w1": i["L0_gnn_W1"],
        "l0_w2": i["L0_gnn_W2"].reshape(2, 128, HID2).transpose(1, 0, 2),
        "l0_w3": i["L0_gnn_W3"].reshape(4, 128, D).transpose(1, 0, 2),
        "l1_wg0": i["L1_gnn_Wg0"], "l1_bg0": i["L1_gnn_bg0"].reshape(1, D),
        "l1_wg1": i["L1_gnn_Wg1"], "l1_bg1": i["L1_gnn_bg1"].reshape(1, D),
        "l1_wihT": i["L1_gnn_Wih"].transpose(2, 0, 1), "l1_whhT": i["L1_gnn_Whh"].transpose(2, 0, 1),
        "l1_bih": i["L1_gnn_bih"].reshape(SKIPS, 4, D).transpose(2, 0, 1),
        "l1_bhh": i["L1_gnn_bhh"].reshape(SKIPS, 4, D).transpose(2, 0, 1),
        "l2_w": i["L2_gnn_W"], "l2_wT": i["L2_gnn_W"].T, "l2_a": cols(i["L2_gnn_a"], 2),
        "l3_w1T": i["L3_gnn_W1"].T,
        "l3_vec1": np.stack([cols(i[f"L3_gnn_{n}"], 2) for n in ("b1", "g1", "be1")], 1),
        "l3_w2T": i["L3_gnn_W2"].T.reshape(2, 128, D).transpose(1, 0, 2),
        "l3_vec2": np.stack([cols(i[f"L3_gnn_{n}"], 1) for n in ("b2", "g2", "be2")], 1),
        "eye": np.eye(128, dtype=np.float32),
    }
    nc = bacc.Bacc("TRN2", target_bir_lowering=False, num_devices=1)
    arrays, args = {}, []
    for name, a in data.items():
        a = np.ascontiguousarray(a)
        arrays[f"in_{name}"] = a
        args.append(nc.dram_tensor(f"in_{name}", a.shape, mb.dt.from_np(a.dtype), kind="ExternalInput").ap())
    out = nc.dram_tensor("out_rows", (GROUPS, N, BH, D), mb.dt.float32, kind="ExternalOutput").ap()
    build_adj_resnorm_d4(nc, *args, out)
    r = run(nc, [arrays], core_ids=[0])
    o = r.results[0]["out_rows"]
    return o.transpose(0, 2, 1, 3).reshape(B, N, D)
```
